# Optimizing a Trainium2 kernel written in Bass

```python
import numpy as np
import jax
import jax.numpy as jnp

def _softmax(x, axis=-1):
    return jax.nn.softmax(x, axis=axis)
def _gelu(x):
    return jax.nn.gelu(x, approximate=True)
def _silu(x):
    return jax.nn.silu(x)
def _sigmoid(x):
    return jax.nn.sigmoid(x)
def _layernorm(x, axis=-1, eps=1e-5):
    m = jnp.mean(x, axis=axis, keepdims=True)
    v = jnp.var(x, axis=axis, keepdims=True)
    return (x - m) / jnp.sqrt(v + eps)
def _scatter_add(tgt, idx, src, axis=0):
    return tgt.at[idx].add(src)
def _segment_sum(src, seg, n):
    return jax.ops.segment_sum(src, seg, n)

kernel_name = 'mk_conv_preact_d1_conv_nhwc32_7d4a07'

def setup_inputs(seed: int = 0):
    np.random.seed(seed)
    _w = jnp.asarray
    def _rec_inputs():
        import jax
        import jax.numpy as jnp
        _gk = jax.random.key(seed)
        x = -0.0001333 + 0.9999 * jax.random.normal(jax.random.fold_in(_gk, 1), (128, 224, 32, 32), jnp.float32)
        return x
    x = _rec_inputs()
    def _L0_conv_setup():
        import jax, jax.numpy as jnp
        import numpy as np
        WS = 8
        HEADS = 8

        def _forward(x, Wq, Wk, Wv, Wo, bo, pos_emb, scale):
            b, c, H, W = x.shape
            nh, nw = (H // WS, W // WS)
            n = nh * nw
            m = WS * WS
            inner = Wq.shape[1]
            d = inner // HEADS
            xh = x.transpose(0, 2, 3, 1)
            q = xh @ Wq
            k = xh @ Wk
            v = xh @ Wv

            def win(t):
                t = t.reshape(b, nh, WS, nw, WS, inner)
                t = t.transpose(0, 1, 3, 2, 4, 5).reshape(b, n, m, inner)
                t = t.transpose(0, 2, 1, 3)
                t = t.reshape(b, m, n, HEADS, d).transpose(0, 1, 3, 2, 4)
                return t
            q2, k2, v2 = (win(q), win(k), win(v))
            q2 = q2 * scale
            sim = jnp.einsum('bmhid,bmhjd->bmhij', q2, k2) + pos_emb
            attn = jax.nn.softmax(sim, axis=-1)
            o = jnp.einsum('bmhij,bmhjd->bmhid', attn, v2)
            o = o.transpose(0, 1, 3, 2, 4).reshape(b, m, n, inner)
            o = o.transpose(0, 2, 1, 3)
            o = o @ Wo + bo
            o = o.reshape(b, nh, nw, WS, WS, c).transpose(0, 1, 3, 2, 4, 5)
            o = o.reshape(b, H, W, c)
            return o.transpose(0, 3, 1, 2)
        key = jax.random.key(seed)
        ks = jax.random.split(key, 8)
        b, dim, H, W = (128, 224, 32, 32)
        inner = 224
        n_win = H // WS * (W // WS)
        return {'x': jax.random.normal(ks[0], (b, dim, H, W), dtype=jnp.float32), 'Wq': jax.random.normal(ks[1], (dim, inner), dtype=jnp.float32) * 0.02, 'Wk': jax.random.normal(ks[2], (dim, inner), dtype=jnp.float32) * 0.02, 'Wv': jax.random.normal(ks[3], (dim, inner), dtype=jnp.float32) * 0.02, 'Wo': jax.random.normal(ks[4], (inner, dim), dtype=jnp.float32) * 0.02, 'bo': jax.random.normal(ks[5], (dim,), dtype=jnp.float32) * 0.02, 'pos_emb': jax.random.normal(ks[6], (1, 1, HEADS, n_win, n_win), dtype=jnp.float32), 'scale': jnp.ones((1,), dtype=jnp.float32)}
    _L0_conv_all = _L0_conv_setup()
    _L0_conv_in = {k: v for k, v in _L0_conv_all.items() if k in ('Wq', 'Wk', 'Wv', 'Wo', 'bo', 'pos_emb', 'scale', )}
    del _L0_conv_all

    return {
        "x": x,
        "L0_conv_Wq": _L0_conv_in["Wq"],
        "L0_conv_Wk": _L0_conv_in["Wk"],
        "L0_conv_Wv": _L0_conv_in["Wv"],
        "L0_conv_Wo": _L0_conv_in["Wo"],
        "L0_conv_bo": _L0_conv_in["bo"],
        "L0_conv_pos_emb": _L0_conv_in["pos_emb"],
        "L0_conv_scale": _L0_conv_in["scale"],
    }

def reference(x, L0_conv_Wq, L0_conv_Wk, L0_conv_Wv, L0_conv_Wo, L0_conv_bo, L0_conv_pos_emb, L0_conv_scale):
    import jax
    import jax.numpy as jnp
    def _L0_conv_ref(x, Wq, Wk, Wv, Wo, bo, pos_emb, scale):
        import jax, jax.numpy as jnp
        import numpy as np
        WS = 8
        HEADS = 8

        def _forward(x, Wq, Wk, Wv, Wo, bo, pos_emb, scale):
            b, c, H, W = x.shape
            nh, nw = (H // WS, W // WS)
            n = nh * nw
            m = WS * WS
            inner = Wq.shape[1]
            d = inner // HEADS
            xh = x.transpose(0, 2, 3, 1)
            q = xh @ Wq
            k = xh @ Wk
            v = xh @ Wv

            def win(t):
                t = t.reshape(b, nh, WS, nw, WS, inner)
                t = t.transpose(0, 1, 3, 2, 4, 5).reshape(b, n, m, inner)
                t = t.transpose(0, 2, 1, 3)
                t = t.reshape(b, m, n, HEADS, d).transpose(0, 1, 3, 2, 4)
                return t
            q2, k2, v2 = (win(q), win(k), win(v))
            q2 = q2 * scale
            sim = jnp.einsum('bmhid,bmhjd->bmhij', q2, k2) + pos_emb
            attn = jax.nn.softmax(sim, axis=-1)
            o = jnp.einsum('bmhij,bmhjd->bmhid', attn, v2)
            o = o.transpose(0, 1, 3, 2, 4).reshape(b, m, n, inner)
            o = o.transpose(0, 2, 1, 3)
            o = o @ Wo + bo
            o = o.reshape(b, nh, nw, WS, WS, c).transpose(0, 1, 3, 2, 4, 5)
            o = o.reshape(b, H, W, c)
            return o.transpose(0, 3, 1, 2)
        return _forward(x, Wq, Wk, Wv, Wo, bo, pos_emb, scale)

    def _gn(v, G=16, eps=1e-5):
        B_, H_, W_, C_ = v.shape
        g = v.reshape(B_, H_, W_, G, C_ // G)
        m = jnp.mean(g, axis=(1, 2, 4), keepdims=True)
        s = jnp.var(g, axis=(1, 2, 4), keepdims=True)
        return ((g - m) / jnp.sqrt(s + eps)).reshape(v.shape)

    def _ln_c(v, eps=1e-6):
        m = jnp.mean(v, axis=-1, keepdims=True)
        s = jnp.var(v, axis=-1, keepdims=True)
        return (v - m) / jnp.sqrt(s + eps)

    def _ln_t(v, eps=1e-5):
        m = jnp.mean(v, axis=-1, keepdims=True)
        s = jnp.var(v, axis=-1, keepdims=True)
        return (v - m) / jnp.sqrt(s + eps)

    def _to_tokens(v):
        B_, H_, W_, C_ = v.shape
        return v.reshape(B_, H_ * W_, C_)
    def _from_tokens(t, like):
        return t.reshape(like.shape)

    x = x + _L0_conv_ref(_gn(x), L0_conv_Wq, L0_conv_Wk, L0_conv_Wv, L0_conv_Wo, L0_conv_bo, L0_conv_pos_emb, L0_conv_scale)
    return x


_drawn_inputs = setup_inputs


def setup_inputs(seed=0):
    import zlib

    import numpy as np

    out = dict(_drawn_inputs(seed))
    spreads = {}
    factors = {'L0_conv_Wq': 4.301, 'L0_conv_Wk': 4.295, 'L0_conv_pos_emb': 2.827}
    for name, (base, spread) in spreads.items():
        noise = np.random.default_rng([zlib.crc32(name.encode()), seed]).standard_normal(out[name].shape)
        drawn = base * np.exp(spread * noise) if base else spread * noise
        out[name] = jnp.asarray(drawn.astype(out[name].dtype))
    for name, factor in factors.items():
        out[name] = (out[name] * factor).astype(out[name].dtype)
    return out
```

```python
from contextlib import ExitStack

import concourse.bass as bass
from concourse import mybir
from concourse.alu_op_type import AluOpType as ALU

ACT = mybir.ActivationFunctionType
AX = mybir.AxisListType
F32 = mybir.dt.float32
F32R = mybir.dt.float32r
I32 = mybir.dt.int32

B, C, HH, WW = 128, 224, 32, 32
WS = 8
NW = HH // WS
TOK = HH * WW
CH, CP = 2, C // 2
HEADS = 8
D = C // HEADS
DP = 32
HG = 2
HPG = HEADS // HG
WIN = NW * NW
PAIRS = 4
TILE = 128
T2 = 2
STEPS = B * TOK // (T2 * TILE)
HALVES = STEPS // 2
HTOK = TOK // 2
G = 16
GROUP_N = C * HH * (WW // G)
EPS = 1e-5
MASK = -1e30
UNIT = T2 * HG * PAIRS
XBUFS = 4

LOAD_LEAD, RSUM_LEAD, SQ_LEAD, RSQ_LEAD, STAT_LEAD = 9, 8, 7, 6, 5
NORM_LEAD, SPLIT_LEAD, PROJ_LEAD = 4, 3, 2
OUT_LAG, FINAL_LAG, STORE_LAG = 2, 3, 6
PERIOD = 4 * XBUFS
FIRST = -LOAD_LEAD
LOOP_AT = 4
ROUNDS = (STEPS - 4 * 3 - LOOP_AT) // PERIOD
LOOP_END = LOOP_AT + ROUNDS * PERIOD
LAST = STEPS + STORE_LAG - 2


def build(nc, x, wq, wk, wv, wo, bo, pos, scale, out):
    ctx = ExitStack()
    with ctx:
        def sb(name, shape, dt=F32):
            return ctx.enter_context(nc.sbuf_tensor(name, shape, dt))

        def sem(name):
            return ctx.enter_context(nc.semaphore(name))

        x_sb = sb("x_sb", [CP, XBUFS, CH, TOK])
        sq = sb("sq", [CP, CH, TOK])
        part = sb("part", [CP, 2 * G])
        st = sb("st", [CP, 2 * G])
        var = sb("var", [CP, G])
        mean_w = sb("mean_w", [CP, WW])
        guess = sb("guess", [CP, G], I32)
        rstd = sb("rstd", [CP, G])
        half_var = sb("half_var", [CP, G])
        three_halves = sb("three_halves", [CP, G])
        newton = sb("newton", [CP, G])
        rstd_t = sb("rstd_t", [CP, TILE])
        xc = sb("xc", [CP, CH, HTOK])
        xn = sb("xn", [CP, CH, HTOK])
        xhi = sb("xhi", [CP, 2, CH, HTOK], F32R)
        xlo = sb("xlo", [CP, 2, CH, HTOK], F32R)
        q_bd = sb("q_bd", [128, 2, HG, HTOK // 32, HPG, 32])
        k_sb = sb("k_sb", [128, 2, HG, HTOK])
        v_sb = sb("v_sb", [128, 4, T2, HG * 128])
        sc = sb("sc", [128, 2, UNIT * 32])
        mx = sb("mx", [128, 2, UNIT])
        sm = sb("sm", [128, 2, UNIT])
        rs = sb("rs", [128, 2, UNIT])
        pt = sb("pt", [128, 2, T2 * HG, 128])
        o_f = sb("o_f", [128, 2, T2 * HG, TILE])
        ohi = sb("ohi", [128, 2, T2 * HG, TILE], F32R)
        olo = sb("olo", [128, 2, T2 * HG, TILE], F32R)
        wqk_f = sb("wqk_f", [CP, CH, 2 * 256])
        wqk = sb("wqk", [CP, 2, CH, 2 * 256], F32R)
        wv_f = sb("wv_f", [CP, CH, 256])
        wv_s = sb("wv_s", [CP, 2, CH, 256], F32R)
        wo_f = sb("wo_f", [128, HG, C])
        wo_s = sb("wo_s", [128, 2, HG, C], F32R)
        bo_sb = sb("bo_sb", [CP, CH])
        scale_sb = sb("scale_sb", [128, 1])
        pos_f = sb("pos_f", [128, HG, 32])
        pos_sb = sb("pos_sb", [128, HG, PAIRS, 32])
        ones = sb("ones", [CP, CP])
        ident = sb("ident", [128, 128])

        ps_qk = ctx.enter_context(nc.psum_tensor("ps_qk", [128, 512], F32))
        ps_vo = ctx.enter_context(nc.psum_tensor("ps_vo", [128, 512], F32))
        ps_s = ctx.enter_context(nc.psum_tensor("ps_s", [128, 512], F32))
        ps_t = ctx.enter_context(nc.psum_tensor("ps_t", [128, 512], F32))
        ps_pv = ctx.enter_context(nc.psum_tensor("ps_pv", [128, PAIRS, 512], F32))

        x_loaded = [sem(f"x_loaded{s}") for s in range(XBUFS)]
        y_stored = [sem(f"y_stored{s}") for s in range(XBUFS)]
        weights_loaded = sem("weights_loaded")
        zeroed = sem("zeroed")
        pos_ready = sem("pos_ready")
        ident_zero = sem("ident_zero")
        ident_ready = sem("ident_ready")
        w_hi = sem("w_hi")
        w_lo = sem("w_lo")
        summed_x = sem("summed_x")
        squared = sem("squared")
        totals = sem("totals")
        stats = sem("stats")
        refined = sem("refined")
        rstd_ready = sem("rstd_ready")
        centred = sem("centred")
        normed = sem("normed")
        x_hi = sem("x_hi")
        x_lo = sem("x_lo")
        qk_done = sem("qk_done")
        qk_kept = sem("qk_kept")
        v_done = sem("v_done")
        v_kept = sem("v_kept")
        scored = sem("scored")
        biased = sem("biased")
        maxed = sem("maxed")
        shifted = sem("shifted")
        exped = sem("exped")
        row_sum = sem("row_sum")
        inverted = sem("inverted")
        probs = sem("probs")
        transposed = sem("transposed")
        pt_kept = sem("pt_kept")
        pv_done = sem("pv_done")
        o_kept = sem("o_kept")
        o_hi = sem("o_hi")
        o_lo = sem("o_lo")
        projected = sem("projected")
        final = sem("final")
        STAT_OPS = 8
        NEWTON = 3
        ROOT_OPS = 4 * NEWTON

        def wait(eng, s, n, i, per_round):
            if isinstance(i, int):
                if n > 0:
                    eng.wait_ge(s, n)
            else:
                assert n > 0
                eng.wait_ge(s, n + i * per_round)

        def rounds(eng, step):
            for t in range(FIRST, LOOP_AT):
                step(t, 0)
            with eng.Fori(0, ROUNDS) as i:
                for t in range(LOOP_AT, LOOP_AT + PERIOD):
                    step(t, i)
            for t in range(LOOP_END, LAST + 1):
                step(t, 0)

        def per_step(eng, s, g, i, each=1):
            wait(eng, s, each * (g + 1), i, each * PERIOD)

        def per_half(eng, s, h, i, each=1):
            wait(eng, s, each * (h + 1), i, each * PERIOD // 2)

        def per_image(eng, s, b, i, each=1):
            wait(eng, s, each * (b + 1), i, each * PERIOD // 4)

        def image_at(t, lead):
            b, r = divmod(t + lead, 4)
            return b if r == 0 and 0 <= b < B else None

        def half_at(t, lead):
            h, r = divmod(t + lead, 2)
            return h if r == 0 and 0 <= h < HALVES else None

        def is_step(g):
            return 0 <= g < STEPS

        block = ctx.enter_context(nc.Block())

        @block.sync
        def _(sp):
            sp.wait_ge(zeroed, 4)
            n_w = 0

            def load_weights(dst, src):
                sp.dma_start(dst, src).then_inc(weights_loaded, 16)

            for kind, w in ((0, wq), (1, wk)):
                for ch in range(CH):
                    load_weights(wqk_f[:, ch, kind * 256:kind * 256 + 256].rearrange("p (h d) -> p h d", d=DP)[:, :, 0:D],
                                 w[ch * CP:(ch + 1) * CP, :].rearrange("p (h d) -> p h d", d=D))
                    n_w += 1
            for ch in range(CH):
                load_weights(wv_f[:, ch, :].rearrange("p (h d) -> p h d", d=DP)[:, :, 0:D],
                             wv[ch * CP:(ch + 1) * CP, :].rearrange("p (h d) -> p h d", d=D))
                n_w += 1
            for hg in range(HG):
                for h in range(HPG):
                    row = (hg * HPG + h) * D
                    load_weights(wo_f[h * DP:h * DP + D, hg, :], wo[row:row + D, :])
                    n_w += 1
                for h in range(HPG):
                    for a in range(2):
                        p0 = h * 32 + a * WIN
                        load_weights(pos_f[p0:p0 + WIN, hg, a * WIN:(a + 1) * WIN], pos[0, 0, hg * HPG + h])
                        n_w += 1
            sp.dma_start(bo_sb[:, :], bo.rearrange("(ch p) -> p ch", p=CP),
                         allow_slow_non_contiguous=True).then_inc(weights_loaded, 16)
            load_weights(scale_sb[:, :], scale.partition_broadcast(128))
            assert n_w + 2 == N_WEIGHTS

            def step(t, i):
                b = image_at(t, -STORE_LAG)
                if b is not None:
                    per_step(sp, final, 4 * b + 3, i)
                    sp.dma_start(out[b + i * XBUFS].rearrange("(ch p) y z -> p ch (y z)", p=CP) if isinstance(i, int)
                                 else out[bass.ds(b + i * XBUFS, 1)].rearrange("o (ch p) y z -> p (o ch) (y z)", p=CP),
                                 x_sb[:, b % XBUFS]).then_inc(y_stored[b % XBUFS], 16)
                b = image_at(t, LOAD_LEAD)
                if b is not None:
                    wait(sp, y_stored[b % XBUFS], 16 * (b // XBUFS), i, 16)
                    sp.dma_start(x_sb[:, b % XBUFS],
                                 x[b + i * XBUFS].rearrange("(ch p) y z -> p ch (y z)", p=CP) if isinstance(i, int)
                                 else x[bass.ds(b + i * XBUFS, 1)].rearrange("o (ch p) y z -> p (o ch) (y z)", p=CP)
                                 ).then_inc(x_loaded[b % XBUFS], 16)

            rounds(sp, step)
            for s in range(XBUFS):
                sp.wait_ge(y_stored[s], 16 * (B // XBUFS))

        @block.tensor
        def _(pe):
            def split_product(dst, w_parts, x_parts, chunks):
                n = 0
                for a, c in ((0, 0), (0, 1), (1, 0)):
                    for ch in range(chunks):
                        last = nc.tensor.matmul(dst, w_parts(a, ch), x_parts(c, ch),
                                                start=(n == 0), stop=(n == 3 * chunks - 1))
                        n += 1
                return last

            x_parts = (xhi, xlo)
            o_parts = (ohi, olo)

            def project_qk(u, j, i):
                h, hg = divmod(u, 2)
                if hg == 0 and j == 0:
                    per_half(pe, x_hi, h, i)
                    per_half(pe, x_lo, h, i)
                n = 2 * u + j
                wait(pe, qk_kept, n, i, 2 * PERIOD)
                c0 = (j * HG + hg) * 128
                split_product(ps_qk[:, :], lambda a, ch: wqk[:, a, ch, c0:c0 + 128],
                              lambda c, ch: x_parts[c][:, h % 2, ch, :], CH).then_inc(qk_done, 1)

            def project_v(g, i):
                h = g // 2
                if is_step(g - PROJ_LEAD - FINAL_LAG):
                    per_step(pe, final, g - PROJ_LEAD - FINAL_LAG, i)
                else:
                    per_step(pe, v_kept, g - 1, i)
                b = image_at(g - PROJ_LEAD, STAT_LEAD)
                if b is not None:
                    wait(pe, stats, STAT_OPS * b + 1, i, STAT_OPS * XBUFS)
                for t2 in range(T2):
                    tok = (g % 2) * 256 + t2 * TILE
                    last = split_product(ps_vo[:, t2 * 256:t2 * 256 + 256],
                                         lambda a, ch: x_parts[a][:, h % 2, ch, tok:tok + TILE],
                                         lambda c, ch: wv_s[:, c, ch, :], CH)
                last.then_inc(v_done, 1)

            def step(t, i):
                if is_step(t):
                    if t % 2 == 0:
                        per_half(pe, qk_kept, t // 2, i, 4)
                    per_step(pe, biased, t - 1, i)
                    for t2 in range(T2):
                        for hg in range(HG):
                            for pr in range(PAIRS):
                                m0 = (t % 2) * 16 + t2 * 8 + pr * 2
                                col = ((t2 * HG + hg) * PAIRS + pr) * 32
                                last = nc.tensor.matmul(
                                    ps_s[:, col:col + 32],
                                    q_bd[:, (t // 2) % 2, hg, m0 // 2].rearrange("p h i -> p (h i)"),
                                    k_sb[:, (t // 2) % 2, hg, m0 * WIN:m0 * WIN + 32], start=True, stop=True)
                    last.then_inc(scored, 1)
                if is_step(t - 1):
                    g = t - 1
                    per_step(pe, probs, g, i)
                    per_step(pe, pt_kept, g - 1, i)
                    for u in range(T2 * HG):
                        last = nc.tensor.transpose(ps_t[:, u * 128:(u + 1) * 128],
                                                   sc[:, g % 2, u * 128:(u + 1) * 128], ident[:, :])
                    last.then_inc(transposed, 1)
                b = image_at(t, STAT_LEAD)
                if b is not None:
                    per_image(pe, summed_x, b, i, 2)
                    per_step(pe, final, t - FINAL_LAG, i)
                    per_step(pe, v_kept, t + PROJ_LEAD - 1, i)
                    nc.tensor.matmul(ps_vo[0:CP, 0:2 * G], ones[:, :], part[:, :],
                                     start=True, stop=True).then_inc(totals, 1)
                u = t + PROJ_LEAD
                if is_step(u):
                    project_qk(u, 0, i)
                    project_v(u, i)
                if is_step(t - 1):
                    g = t - 1
                    per_step(pe, pt_kept, g, i)
                    per_step(pe, v_kept, g, i)
                    per_step(pe, o_kept, g - 1, i)
                    for un in range(T2 * HG):
                        t2, hg = divmod(un, HG)
                        for pr in range(PAIRS):
                            last = nc.tensor.matmul(ps_pv[:, pr, un * 128:(un + 1) * 128],
                                                    v_sb[pr * 32:pr * 32 + 32, g % 4, t2, hg * 128:(hg + 1) * 128],
                                                    pt[pr * 32:pr * 32 + 32, g % 2, un, :], start=True, stop=True)
                    last.then_inc(pv_done, 1)
                if is_step(u):
                    project_qk(u, 1, i)
                g = t - OUT_LAG
                if is_step(g):
                    per_step(pe, o_hi, g, i)
                    per_step(pe, o_lo, g, i)
                    last_v = min(t + PROJ_LEAD, STEPS - 1)
                    per_step(pe, v_kept, last_v, i)
                    if not is_step(u):
                        per_step(pe, final, g - 1, i)
                    for ch in range(CH):
                        last = split_product(ps_vo[0:CP, ch * 256:ch * 256 + 256],
                                             lambda a, hg: wo_s[:, a, hg, ch * CP:(ch + 1) * CP],
                                             lambda c, hg: o_parts[c][:, g % 2, hg::HG, :], HG)
                    last.then_inc(projected, 1)

            pe.wait_ge(ident_ready, 1)
            pe.wait_ge(zeroed, 7)
            pe.wait_ge(w_hi, 3)
            pe.wait_ge(w_lo, 3)
            rounds(pe, step)

        @block.scalar
        def _(act):
            act.wait_ge(weights_loaded, 16 * N_WEIGHTS)
            for hi, full in ((wqk, wqk_f), (wv_s, wv_f), (wo_s, wo_f)):
                nc.scalar.activation(hi[:, 0], full[:, :, :], ACT.Copy).then_inc(w_hi, 1)

            def keep_qk(u, j, i):
                h, hg = divmod(u, 2)
                wait(act, qk_done, 2 * u + j + 1, i, 2 * PERIOD)
                if j == 0 and hg == 0:
                    per_step(act, scored, 2 * h - 3, i)
                if j == 0:
                    for hd in range(HPG):
                        p = slice(hd * DP, hd * DP + DP)
                        last = nc.scalar.activation(q_bd[p, h % 2, hg, :, hd, :],
                                                    ps_qk[p, :].rearrange("p (m i) -> p m i", i=32),
                                                    ACT.Copy, scale=scale_sb[p, :])
                else:
                    last = nc.scalar.activation(k_sb[:, h % 2, hg, :], ps_qk[:, :], ACT.Copy)
                last.then_inc(qk_kept, 1)

            def step(t, i):
                if is_step(t - 1):
                    g = t - 1
                    per_step(act, transposed, g, i)
                    per_step(act, pv_done, g - 2, i)
                    nc.scalar.activation(pt[:, g % 2], ps_t[:, :].rearrange("p (u c) -> p u c", c=128),
                                         ACT.Copy).then_inc(pt_kept, 1)
                u = t + PROJ_LEAD
                if is_step(u):
                    keep_qk(u, 0, i)
                if is_step(t):
                    per_step(act, shifted, t, i)
                    nc.scalar.activation(sc[:, t % 2], sc[:, t % 2], ACT.Exp).then_inc(exped, 1)
                h = half_at(t, SPLIT_LEAD)
                if h is not None:
                    per_half(act, normed, h, i)
                    per_half(act, qk_done, h - 2, i, 4)
                    per_step(act, v_done, 2 * (h - 2) + 1, i)
                    nc.scalar.activation(xhi[:, h % 2], xn[:, :, :], ACT.Copy).then_inc(x_hi, 1)
                b = image_at(t, SQ_LEAD)
                if b is not None:
                    wait(act, x_loaded[b % XBUFS], 16 * (b // XBUFS + 1), i, 16)
                    per_image(act, summed_x, b - 1, i, 2)
                    nc.scalar.activation(sq[:, :, :], x_sb[:, b % XBUFS], ACT.Square).then_inc(squared, 1)
                if is_step(t - 1):
                    g = t - 1
                    per_step(act, pv_done, g, i)
                    per_step(act, projected, g - 2, i)
                    for hd in range(HPG):
                        p = slice(hd * DP, hd * DP + DP)
                        last = nc.scalar.activation(
                            o_f[p, g % 2].rearrange("p u (pr i) -> p u pr i", i=32),
                            ps_pv[p, :, :].rearrange("p pr (u h i) -> p u pr h i", u=T2 * HG, h=HPG)[:, :, :, hd, :],
                            ACT.Copy)
                    last.then_inc(o_kept, 1)
                if is_step(u):
                    keep_qk(u, 1, i)

            act.wait_ge(zeroed, 7)
            rounds(act, step)

        @block.vector
        def _(dve):
            nc.vector.memset(wqk_f[:, :, :], 0.0).then_inc(zeroed, 1)
            nc.vector.memset(wv_f[:, :, :], 0.0).then_inc(zeroed, 1)
            nc.vector.memset(wo_f[:, :, :], 0.0).then_inc(zeroed, 1)
            nc.vector.memset(pos_f[:, :, :], MASK).then_inc(zeroed, 1)
            nc.vector.memset(ones[:, :], 1.0).then_inc(zeroed, 1)
            nc.vector.memset(three_halves[:, :], 1.5).then_inc(zeroed, 1)
            nc.vector.memset(q_bd[:, :, :, :, :, :].rearrange("p a b c d e -> p (a b c d e)"), 0.0).then_inc(zeroed, 1)
            dve.wait_ge(w_hi, 3)
            dve.wait_ge(weights_loaded, 16 * N_WEIGHTS)
            nc.vector.tensor_copy(pos_sb[:, :, :, :], pos_f[:, :, :].unsqueeze(2).broadcast_to((128, HG, PAIRS, 32))).then_inc(pos_ready, 1)
            dve.wait_ge(pos_ready, 1)
            for parts, full in ((wqk, wqk_f), (wv_s, wv_f), (wo_s, wo_f)):
                nc.vector.tensor_tensor(parts[:, 1], full[:, :, :], parts[:, 0], ALU.subtract).then_inc(w_lo, 1)

            def stat_op(b, i, n, make):
                wait(dve, stats, STAT_OPS * b + n, i, STAT_OPS * XBUFS)
                make().then_inc(stats, 1)

            def stat_ops(b, i):
                mean, msq = st[:, 0:G], st[:, G:2 * G]
                two = (CP, G, WW // G)
                yield lambda: nc.vector.tensor_scalar(st[:, :], ps_vo[0:CP, 0:2 * G], 1.0 / GROUP_N, None, ALU.mult)
                yield lambda: nc.vector.tensor_copy(mean_w[:, :].rearrange("p (g w) -> p g w", g=G),
                                                    mean.unsqueeze(2).broadcast_to(two))
                yield lambda: nc.vector.scalar_tensor_tensor(var[:, :], mean, -1.0, mean, ALU.mult, ALU.mult)
                yield lambda: nc.vector.tensor_tensor(var[:, :], var[:, :], msq, ALU.add)
                yield lambda: nc.vector.tensor_scalar(var[:, :], var[:, :], 0.0, EPS, ALU.max, ALU.add)
                yield lambda: nc.vector.tensor_scalar(half_var[:, :], var[:, :], 0.5, None, ALU.mult)
                yield lambda: nc.vector.tensor_scalar(guess[:, :], var[:, :].bitcast(I32), 1, None, ALU.logical_shift_right)
                yield lambda: nc.vector.tensor_scalar(guess[:, :], guess[:, :], -1.0, float(0x5F3759DF), ALU.mult, ALU.add)

            def step(t, i):
                g = t - FINAL_LAG
                if is_step(g):
                    b = g // 4
                    per_step(dve, projected, g, i)
                    for ch in range(CH):
                        xs = x_sb[:, b % XBUFS, ch].rearrange("p (nh r nw c) -> p r nh nw c", nh=NW, r=WS, nw=NW)
                        for t2 in range(T2):
                            xr = xs[:, (g % 4) * T2 + t2]
                            c0 = ch * 256 + t2 * TILE
                            last = nc.vector.scalar_tensor_tensor(
                                xr, ps_vo[0:CP, c0:c0 + TILE].rearrange("p (c nh nw) -> p nh nw c", c=WS, nh=NW),
                                bo_sb[:, ch:ch + 1], xr, ALU.add, ALU.add)
                    last.then_inc(final, 1)
                todo = []
                bs = image_at(t, STAT_LEAD)
                if bs is not None:
                    todo = [lambda n=n, m=m: stat_op(bs, i, n, m) for n, m in enumerate(stat_ops(bs, i))]
                    per_image(dve, totals, bs, i)
                    per_half(dve, normed, 2 * bs - 1, i)
                    per_image(dve, rstd_ready, bs - 1, i)
                    todo.pop(0)()
                if is_step(t):
                    per_step(dve, scored, t, i)
                    nc.vector.tensor_tensor(
                        sc[:, t % 2].rearrange("p (t2 c) -> p t2 c", t2=T2),
                        ps_s[:, :].rearrange("p (t2 c) -> p t2 c", t2=T2),
                        pos_sb[:, :, :, :].rearrange("p hg pr c -> p (hg pr c)").unsqueeze(1).broadcast_to((128, T2, HG * PAIRS * 32)),
                        ALU.add).then_inc(biased, 1)
                if todo:
                    todo.pop(0)()
                rows = sc[:, t % 2].rearrange("p (u c) -> p u c", c=32)
                if is_step(t):
                    per_step(dve, biased, t, i)
                    nc.vector.reduce_max(mx[:, t % 2], rows, axis=AX.X).then_inc(maxed, 1)
                if todo:
                    todo.pop(0)()
                g = t - OUT_LAG
                if is_step(g):
                    per_step(dve, o_kept, g, i)
                    per_step(dve, projected, g - 2, i)
                    nc.vector.tensor_copy(ohi[:, g % 2], o_f[:, g % 2]).then_inc(o_hi, 1)
                if todo:
                    todo.pop(0)()
                if is_step(t):
                    per_step(dve, maxed, t, i)
                    nc.vector.tensor_tensor(rows, rows, mx[:, t % 2].unsqueeze(2).broadcast_to((128, UNIT, 32)),
                                            ALU.subtract).then_inc(shifted, 1)
                while todo:
                    todo.pop(0)()
                h = half_at(t, NORM_LEAD)
                if h is not None:
                    b, hh = divmod(h, 2)
                    per_image(dve, stats, b, i, STAT_OPS)
                    if hh == 0:
                        wait(dve, x_loaded[b % XBUFS], 16 * (b // XBUFS + 1), i, 16)
                    per_half(dve, normed, h - 1, i)
                    for ch in range(CH):
                        nc.vector.tensor_tensor(
                            xc[:, ch, :].rearrange("p (r nh w) -> p nh r w", nh=NW, w=WW),
                            x_sb[:, b % XBUFS, ch].rearrange("p (nh r w) -> p nh r w", nh=NW, r=WS)[:, :, hh * 4:hh * 4 + 4, :],
                            mean_w[:, :].unsqueeze(1).unsqueeze(1).broadcast_to((CP, NW, WS // 2, WW)),
                            ALU.subtract).then_inc(centred, 1)
                    per_half(dve, x_hi, h - 1, i)
                    per_half(dve, x_lo, h - 1, i)
                    per_half(dve, centred, h, i, CH)
                    per_image(dve, rstd_ready, b, i)
                    nc.vector.tensor_tensor(
                        xn[:, :, :].rearrange("p ch (r c n) -> p (ch r) c n", c=WS, n=WIN),
                        xc[:, :, :].rearrange("p ch (r n c) -> p (ch r) c n", c=WS, n=WIN),
                        rstd_t[:, :].rearrange("p (c n) -> p c n", n=WIN).unsqueeze(1).broadcast_to((CP, CH * WS // 2, WS, WIN)),
                        ALU.mult).then_inc(normed, 1)
                by_group = "p (y g w) -> p g y w"
                b = image_at(t, RSUM_LEAD)
                if b is not None:
                    wait(dve, x_loaded[b % XBUFS], 16 * (b // XBUFS + 1), i, 16)
                    per_image(dve, totals, b - 1, i)
                    nc.vector.tensor_reduce(part[:, 0:G], x_sb[:, b % XBUFS].rearrange("p ch n -> p (ch n)")
                                            .rearrange(by_group, g=G, w=WW // G),
                                            AX.XY, ALU.add).then_inc(summed_x, 1)
                b = image_at(t, RSQ_LEAD)
                if b is not None:
                    per_image(dve, squared, b, i)
                    nc.vector.tensor_reduce(part[:, G:2 * G], sq[:, :, :].rearrange("p ch n -> p (ch n)")
                                            .rearrange(by_group, g=G, w=WW // G),
                                            AX.XY, ALU.add).then_inc(summed_x, 1)
                u = t + PROJ_LEAD
                if is_step(u):
                    per_step(dve, v_done, u, i)
                    per_step(dve, pv_done, u - 4, i)
                    nc.vector.tensor_copy(v_sb[:, u % 4], ps_vo[:, :].rearrange("p (t c) -> p t c", t=T2)).then_inc(v_kept, 1)
                if is_step(t):
                    per_step(dve, exped, t, i)
                    nc.vector.reduce_sum(sm[:, t % 2], rows, axis=AX.X).then_inc(row_sum, 1)
                    per_step(dve, row_sum, t, i)
                    nc.vector.reciprocal(rs[:, t % 2], sm[:, t % 2]).then_inc(inverted, 1)

            rounds(dve, step)

        @block.gpsimd
        def _(pool):
            nc.gpsimd.memset(ident[:, :], 0.0).then_inc(ident_zero, 1)
            pool.wait_ge(ident_zero, 1)
            nc.gpsimd.affine_select(out=ident[:, :], in_=ident[:, :], compare_op=ALU.not_equal, fill=1.0,
                                    base=0, pattern=[[-1, 128]], channel_multiplier=1).then_inc(ident_ready, 1)

            def root(b, i):
                per_image(pool, stats, b, i, STAT_OPS)
                per_half(pool, normed, 2 * b - 1, i)
                n = 0
                y = guess[:, :].bitcast(F32)
                for k in range(NEWTON):
                    for make in (lambda: nc.gpsimd.tensor_tensor(newton[:, :], y, y, ALU.mult),
                                 lambda: nc.gpsimd.tensor_tensor(newton[:, :], newton[:, :], half_var[:, :], ALU.mult),
                                 lambda: nc.gpsimd.tensor_tensor(newton[:, :], three_halves[:, :], newton[:, :], ALU.subtract),
                                 lambda: nc.gpsimd.tensor_tensor(rstd[:, :], y, newton[:, :], ALU.mult)):
                        wait(pool, refined, ROOT_OPS * b + n, i, ROOT_OPS * XBUFS)
                        make().then_inc(refined, 1)
                        n += 1
                    y = rstd[:, :]
                per_image(pool, refined, b, i, ROOT_OPS)
                c2 = WS // 2
                by_token = (CP, c2, 2 * NW, NW)
                nc.gpsimd.tensor_tensor(
                    rstd_t[:, :].rearrange("p (c x nw) -> p c x nw", c=c2, nw=NW),
                    rstd[:, :].rearrange("p (nw c) -> p c nw", c=c2).unsqueeze(2).broadcast_to(by_token),
                    ones[:, 0:1].unsqueeze(1).unsqueeze(1).broadcast_to(by_token), ALU.mult).then_inc(rstd_ready, 1)

            def step(t, i):
                g = t - OUT_LAG
                if is_step(g):
                    per_step(pool, o_hi, g, i)
                    per_step(pool, projected, g - 2, i)
                    nc.gpsimd.tensor_tensor(olo[:, g % 2], o_f[:, g % 2], ohi[:, g % 2],
                                            ALU.subtract).then_inc(o_lo, 1)
                h = half_at(t, SPLIT_LEAD)
                if h is not None:
                    per_half(pool, x_hi, h, i)
                    nc.gpsimd.tensor_tensor(xlo[:, h % 2], xn[:, :, :], xhi[:, h % 2],
                                            ALU.subtract).then_inc(x_lo, 1)
                b = image_at(t, STAT_LEAD)
                if b is not None:
                    root(b, i)
                if is_step(t):
                    per_step(pool, inverted, t, i)
                    rows = sc[:, t % 2].rearrange("p (u c) -> p u c", c=32)
                    nc.gpsimd.tensor_tensor(rows, rows, rs[:, t % 2].unsqueeze(2).broadcast_to((128, UNIT, 32)),
                                            ALU.mult).then_inc(probs, 1)

            pool.wait_ge(zeroed, 7)
            rounds(pool, step)


N_WEIGHTS = 2 * CH + CH + HG * (HPG + 2 * HPG) + 2

_INS = ["x", "L0_conv_Wq", "L0_conv_Wk", "L0_conv_Wv", "L0_conv_Wo", "L0_conv_bo", "L0_conv_pos_emb", "L0_conv_scale"]


def kernel(**inputs):
    import numpy as np
    import concourse.bacc as bacc
    from concourse.bass_utils import run_bass_kernel_spmd

    nc = bacc.Bacc("TRN2", target_bir_lowering=False, num_devices=1)
    arrays, args = {}, []
    for name in _INS:
        a = np.ascontiguousarray(inputs[name])
        arrays[f"in_{name}"] = a
        args.append(nc.dram_tensor(f"in_{name}", a.shape, F32, kind="ExternalInput").ap())
    out = nc.dram_tensor("out_y", (B, C, HH, WW), F32, kind="ExternalOutput").ap()
    build(nc, *args, out)
    r = run_bass_kernel_spmd(nc, [arrays], core_ids=[0])
    return r.results[0]["out_y"]
```

```python
from contextlib import ExitStack

import concourse.bass as bass
from concourse import mybir
from concourse.alu_op_type import AluOpType as ALU

ACT = mybir.ActivationFunctionType
AX = mybir.AxisListType
F32 = mybir.dt.float32
F32R = mybir.dt.float32r
I32 = mybir.dt.int32
F16 = mybir.dt.float16

B, C, HH, WW = 128, 224, 32, 32
WS = 8
NW = HH // WS
TOK = HH * WW
CH, CP = 2, C // 2
HEADS = 8
D = C // HEADS
DP = 32
HG = 2
HPG = HEADS // HG
WIN = NW * NW
PAIRS = 4
TILE = 128
T2 = 2
STEPS = B * TOK // (T2 * TILE)
HALVES = STEPS // 2
HTOK = TOK // 2
G = 16
GROUP_N = C * HH * (WW // G)
EPS = 1e-5
MASK = -1e30
X_SCALE = 16.0
PASSES = ((0, 0), (0, 1), (1, 0))
UNIT = T2 * HG * PAIRS
XBUFS = 4
VBUFS = 8

LOAD_LEAD, RSUM_LEAD, SQ_LEAD, RSQ_LEAD, STAT_LEAD = 10, 9, 9, 8, 7
CENTRE_LEAD, NORM_LEAD, SPLIT_LEAD, PROJ_LEAD = 6, 5, 4, 3
OUT_LAG, FINAL_LAG, STORE_LAG = 2, 3, 6
PERIOD = 4 * XBUFS
FIRST = -LOAD_LEAD
LOOP_AT = 4
ROUNDS = (STEPS - LOAD_LEAD - LOOP_AT) // PERIOD
LOOP_END = LOOP_AT + ROUNDS * PERIOD
LAST = STEPS + STORE_LAG - 2


def build(nc, x, wq, wk, wv, wo, bo, pos, scale, out):
    ctx = ExitStack()
    with ctx:
        def sb(name, shape, dt=F32):
            return ctx.enter_context(nc.sbuf_tensor(name, shape, dt))

        def sem(name):
            return ctx.enter_context(nc.semaphore(name))

        x_sb = sb("x_sb", [CP, XBUFS, CH, TOK])
        sq = sb("sq", [CP, CH, TOK])
        part = sb("part", [CP, 2 * G])
        st = sb("st", [CP, 2 * G])
        var = sb("var", [CP, G])
        mean_w = sb("mean_w", [CP, WW])
        guess = sb("guess", [CP, G], I32)
        rstd = sb("rstd", [CP, G])
        half_var = sb("half_var", [CP, G])
        three_halves = sb("three_halves", [CP, G])
        newton = sb("newton", [CP, G])
        rstd_t = sb("rstd_t", [CP, TILE])
        xc = sb("xc", [CP, CH, HTOK])
        xn = sb("xn", [CP, CH, HTOK])
        xhi = sb("xhi", [CP, 2, CH, HTOK], F16)
        xlo = sb("xlo", [CP, 2, CH, HTOK], F16)
        q_cut = sb("q_cut", [128, HG, 2, HTOK], F16)
        q_bd = sb("q_bd", [128, 2, HG, 2, HPG, HTOK], F16)
        k_sb = sb("k_sb", [128, 2, HG, 2, HTOK], F16)
        v_f = sb("v_f", [128, T2 * C])
        v_sb = sb("v_sb", [128, VBUFS, 2, T2 * HG * 128], F16)
        sc = sb("sc", [128, 2, UNIT * 32])
        mx = sb("mx", [128, 2, UNIT])
        sm = sb("sm", [128, 2, UNIT])
        rs = sb("rs", [128, 2, UNIT])
        pt = sb("pt", [128, 2, 2, T2 * HG * 128], F16)
        o_f = sb("o_f", [128, 2, T2 * HG, TILE])
        ohi = sb("ohi", [128, 2, T2 * HG, WIN, WS], F32R)
        olo = sb("olo", [128, 2, T2 * HG, WIN, WS], F32R)
        wqk_f = sb("wqk_f", [CP, CH, 2 * 256])
        wqk = sb("wqk", [CP, 2, CH, 2 * 256], F16)
        wv_f = sb("wv_f", [CP, CH, C])
        wv_s = sb("wv_s", [CP, 2, CH, C], F16)
        wo_f = sb("wo_f", [128, HG, C])
        wo_s = sb("wo_s", [128, 2, HG, C], F32R)
        bo_sb = sb("bo_sb", [CP, CH])
        scale_sb = sb("scale_sb", [128, 1])
        w_max = sb("w_max", [128, 3])
        w_top = sb("w_top", [128, 3])
        w_pow = sb("w_pow", [128, 3], I32)
        alpha = sb("alpha", [128, 3], I32)
        unscale = sb("unscale", [128, 3])
        s_scale = sb("s_scale", [128, 1])
        pos_f = sb("pos_f", [128, HG, 32])
        pos_sb = sb("pos_sb", [128, HG, PAIRS, 32])
        ones = sb("ones", [CP, CP])
        x_scale = sb("x_scale", [CP, 1])
        ident = sb("ident", [128, 128])

        ps_qk = ctx.enter_context(nc.psum_tensor("ps_qk", [128, 512], F32))
        ps_vo = ctx.enter_context(nc.psum_tensor("ps_vo", [128, 512], F32))
        ps_s = ctx.enter_context(nc.psum_tensor("ps_s", [128, 512], F32))
        ps_t = ctx.enter_context(nc.psum_tensor("ps_t", [128, 512], F32))
        ps_pv = ctx.enter_context(nc.psum_tensor("ps_pv", [128, PAIRS, 512], F32))

        x_loaded = [sem(f"x_loaded{s}") for s in range(XBUFS)]
        y_stored = [sem(f"y_stored{s}") for s in range(XBUFS)]
        weights_loaded = sem("weights_loaded")
        zeroed = sem("zeroed")
        pos_ready = sem("pos_ready")
        ident_zero = sem("ident_zero")
        v_zeroed = sem("v_zeroed")
        ident_ready = sem("ident_ready")
        w_absmax = sem("w_absmax")
        w_allmax = sem("w_allmax")
        w_factor = sem("w_factor")
        w_scaled = sem("w_scaled")
        w_hi = sem("w_hi")
        w_lo = sem("w_lo")
        summed_x = sem("summed_x")
        squared = sem("squared")
        totals = sem("totals")
        stats = sem("stats")
        refined = sem("refined")
        rstd_ready = sem("rstd_ready")
        centred = sem("centred")
        normed = sem("normed")
        x_hi = sem("x_hi")
        x_lo = sem("x_lo")
        qk_done = sem("qk_done")
        qk_hi = sem("qk_hi")
        qk_kept = sem("qk_kept")
        q_placed = [sem(f"q_placed{hg}") for hg in range(HG)]
        v_done = sem("v_done")
        v_out = sem("v_out")
        v_hi = sem("v_hi")
        v_kept = sem("v_kept")
        scored = sem("scored")
        biased = sem("biased")
        maxed = sem("maxed")
        shifted = sem("shifted")
        exped = sem("exped")
        row_sum = sem("row_sum")
        inverted = sem("inverted")
        probs = sem("probs")
        transposed = sem("transposed")
        pt_hi = sem("pt_hi")
        pt_kept = sem("pt_kept")
        pv_done = sem("pv_done")
        o_kept = sem("o_kept")
        o_hi = sem("o_hi")
        o_lo = sem("o_lo")
        projected = sem("projected")
        final = sem("final")
        STAT_OPS = 8
        NEWTON = 3
        ROOT_OPS = 4 * NEWTON

        def wait(eng, s, n, i, per_round):
            if isinstance(i, int):
                if n > 0:
                    eng.wait_ge(s, n)
            else:
                assert n > 0
                eng.wait_ge(s, n + i * per_round)

        def rounds(eng, step):
            for t in range(FIRST, LOOP_AT):
                step(t, 0)
            with eng.Fori(0, ROUNDS) as i:
                for t in range(LOOP_AT, LOOP_AT + PERIOD):
                    step(t, i)
            for t in range(LOOP_END, LAST + 1):
                step(t, 0)

        def per_step(eng, s, g, i, each=1):
            wait(eng, s, each * (g + 1), i, each * PERIOD)

        def per_half(eng, s, h, i, each=1):
            wait(eng, s, each * (h + 1), i, each * PERIOD // 2)

        def per_image(eng, s, b, i, each=1):
            wait(eng, s, each * (b + 1), i, each * PERIOD // 4)

        def image_at(t, lead):
            b, r = divmod(t + lead, 4)
            return b if r == 0 and 0 <= b < B else None

        def half_at(t, lead):
            h, r = divmod(t + lead, 2)
            return h if r == 0 and 0 <= h < HALVES else None

        def is_step(g):
            return 0 <= g < STEPS

        def in_x_order(ap):
            return ap.rearrange("p u (c n) -> p u n c", c=WS)

        block = ctx.enter_context(nc.Block())

        @block.sync
        def _(sp):
            sp.wait_ge(zeroed, 8)
            n_w = 0

            def load_weights(dst, src):
                sp.dma_start(dst, src).then_inc(weights_loaded, 16)

            for kind, w in ((0, wq), (1, wk)):
                for ch in range(CH):
                    load_weights(wqk_f[:, ch, kind * 256:kind * 256 + 256].rearrange("p (h d) -> p h d", d=DP)[:, :, 0:D],
                                 w[ch * CP:(ch + 1) * CP, :].rearrange("p (h d) -> p h d", d=D))
                    n_w += 1
            for ch in range(CH):
                load_weights(wv_f[:, ch, :], wv[ch * CP:(ch + 1) * CP, :])
                n_w += 1
            for hg in range(HG):
                for h in range(HPG):
                    row = (hg * HPG + h) * D
                    load_weights(wo_f[h * DP:h * DP + D, hg, :], wo[row:row + D, :])
                    n_w += 1
                for h in range(HPG):
                    for a in range(2):
                        p0 = h * 32 + a * WIN
                        load_weights(pos_f[p0:p0 + WIN, hg, a * WIN:(a + 1) * WIN], pos[0, 0, hg * HPG + h])
                        n_w += 1
            sp.dma_start(bo_sb[:, :], bo.rearrange("(ch p) -> p ch", p=CP),
                         allow_slow_non_contiguous=True).then_inc(weights_loaded, 16)
            load_weights(scale_sb[:, :], scale.partition_broadcast(128))
            assert n_w + 2 == N_WEIGHTS

            def step(t, i):
                b = image_at(t, -STORE_LAG)
                if b is not None:
                    per_step(sp, final, 4 * b + 3, i)
                    sp.dma_start(out[b + i * XBUFS].rearrange("(ch p) y z -> p ch (y z)", p=CP) if isinstance(i, int)
                                 else out[bass.ds(b + i * XBUFS, 1)].rearrange("o (ch p) y z -> p (o ch) (y z)", p=CP),
                                 x_sb[:, b % XBUFS]).then_inc(y_stored[b % XBUFS], 16)
                u = t + PROJ_LEAD
                if is_step(u):
                    h, hg = divmod(u, 2)
                    wait(sp, qk_kept, 2 * u + 1, i, 2 * PERIOD)
                    for hd in range(HPG):
                        p = slice(hd * DP, hd * DP + DP)
                        sp.dma_start(q_bd[p, h % 2, hg, :, hd, :], q_cut[p, hg]).then_inc(q_placed[hg], 16)
                b = image_at(t, LOAD_LEAD)
                if b is not None:
                    wait(sp, y_stored[b % XBUFS], 16 * (b // XBUFS), i, 16)
                    sp.dma_start(x_sb[:, b % XBUFS],
                                 x[b + i * XBUFS].rearrange("(ch p) y z -> p ch (y z)", p=CP) if isinstance(i, int)
                                 else x[bass.ds(b + i * XBUFS, 1)].rearrange("o (ch p) y z -> p (o ch) (y z)", p=CP)
                                 ).then_inc(x_loaded[b % XBUFS], 16)

            rounds(sp, step)
            for s in range(XBUFS):
                sp.wait_ge(y_stored[s], 16 * (B // XBUFS))

        @block.tensor
        def _(pe):
            def split_product(dst, w_parts, x_parts, chunks):
                n = 0
                for a, c in PASSES:
                    for ch in range(chunks):
                        last = nc.tensor.matmul(dst, w_parts(a, ch), x_parts(c, ch),
                                                start=(n == 0), stop=(n == 3 * chunks - 1))
                        n += 1
                return last

            x_parts = (xhi, xlo)
            o_parts = (ohi, olo)

            def project_qk(u, j, i):
                h, hg = divmod(u, 2)
                if hg == 0 and j == 0:
                    per_half(pe, x_hi, h, i)
                    per_half(pe, x_lo, h, i)
                n = 2 * u + j
                wait(pe, qk_kept, n, i, 2 * PERIOD)
                c0 = (j * HG + hg) * 128
                split_product(ps_qk[:, :], lambda a, ch: wqk[:, a, ch, c0:c0 + 128],
                              lambda c, ch: x_parts[c][:, h % 2, ch, :], CH).then_inc(qk_done, 1)

            def project_v(g, i):
                h = g // 2
                if is_step(g - PROJ_LEAD - FINAL_LAG):
                    per_step(pe, final, g - PROJ_LEAD - FINAL_LAG, i)
                else:
                    per_step(pe, v_hi, g - 1, i)
                for t2 in range(T2):
                    tok = (g % 2) * 256 + t2 * TILE
                    last = split_product(ps_vo[:, t2 * 256:t2 * 256 + C],
                                         lambda a, ch: x_parts[a][:, h % 2, ch, tok:tok + TILE],
                                         lambda c, ch: wv_s[:, c, ch, :], CH)
                last.then_inc(v_done, 1)

            def weigh_values(g, t2):
                for un in (t2 * HG, t2 * HG + 1):
                    cols = slice(un * 128, un * 128 + 128)
                    for n, (a, c) in enumerate(PASSES):
                        for pr in range(PAIRS):
                            p = slice(pr * 32, pr * 32 + 32)
                            last = nc.tensor.matmul(ps_pv[:, pr, cols], v_sb[p, g % VBUFS, a, cols], pt[p, g % 2, c, cols],
                                                    start=(n == 0), stop=(n == 2))
                return last

            def step(t, i):
                if is_step(t):
                    if t % 2 == 0:
                        per_half(pe, q_placed[0], t // 2, i, 16 * HPG)
                        per_half(pe, q_placed[1], t // 2, i, 16 * HPG)
                        per_half(pe, qk_kept, t // 2, i, 4)
                    per_step(pe, biased, t - 1, i)
                    b = image_at(t - 1, STAT_LEAD)
                    if b is not None:
                        wait(pe, stats, STAT_OPS * b + 1, i, STAT_OPS * XBUFS)
                    for t2 in range(T2):
                        for hg in range(HG):
                            for pr in range(PAIRS):
                                pair = ((t % 2) * T2 + t2) * PAIRS + pr
                                col = ((t2 * HG + hg) * PAIRS + pr) * 32
                                for n, (a, c) in enumerate(PASSES):
                                    last = nc.tensor.matmul(
                                        ps_s[:, col:col + 32],
                                        q_bd[:, (t // 2) % 2, hg, a].rearrange("p h (c r) -> p (h c) r", r=HTOK // 32)[:, :, pair],
                                        k_sb[:, (t // 2) % 2, hg, c, pair * 32:pair * 32 + 32],
                                        start=(n == 0), stop=(n == 2))
                    last.then_inc(scored, 1)
                if is_step(t - 1):
                    g = t - 1
                    per_step(pe, probs, g, i)
                    per_step(pe, pt_kept, g - 1, i)
                    for u in range(T2 * HG):
                        last = nc.tensor.transpose(ps_t[:, u * 128:(u + 1) * 128],
                                                   sc[:, g % 2, u * 128:(u + 1) * 128], ident[:, :])
                    last.then_inc(transposed, 1)
                u = t + PROJ_LEAD
                if is_step(u):
                    project_qk(u, 0, i)
                    project_v(u, i)
                b = image_at(t, STAT_LEAD)
                if b is not None:
                    per_image(pe, summed_x, b, i, 2)
                    per_step(pe, biased, t, i)
                    nc.tensor.matmul(ps_s[0:CP, 0:2 * G], ones[:, :], part[:, :],
                                     start=True, stop=True).then_inc(totals, 1)
                if is_step(t - 1):
                    per_step(pe, pt_kept, t - 1, i)
                    per_step(pe, v_kept, t - 1, i)
                    per_step(pe, o_kept, t - 2, i)
                    weigh_values(t - 1, 0)
                if is_step(u):
                    project_qk(u, 1, i)
                if is_step(t - 1):
                    weigh_values(t - 1, 1).then_inc(pv_done, 1)
                g = t - OUT_LAG
                if is_step(g):
                    per_step(pe, o_hi, g, i)
                    per_step(pe, o_lo, g, i)
                    last_v = min(t + PROJ_LEAD, STEPS - 1)
                    per_step(pe, v_hi, last_v, i)
                    if not is_step(u):
                        per_step(pe, final, g - 1, i)
                    for ch in range(CH):
                        last = split_product(ps_vo[0:CP, ch * 256:ch * 256 + 256],
                                             lambda a, hg: wo_s[:, a, hg, ch * CP:(ch + 1) * CP],
                                             lambda c, hg: o_parts[c][:, g % 2, hg::HG].rearrange("p t (nh nw) c -> p nh t (nw c)", nh=NW), HG)
                    last.then_inc(projected, 1)

            pe.wait_ge(ident_ready, 1)
            pe.wait_ge(zeroed, 8)
            pe.wait_ge(w_hi, 3)
            pe.wait_ge(w_lo, 3)
            rounds(pe, step)

        @block.scalar
        def _(act):
            act.wait_ge(w_scaled, 4)
            act.wait_ge(v_zeroed, 1)
            for hi, full in ((wqk, wqk_f), (wv_s, wv_f), (wo_s, wo_f)):
                nc.scalar.activation(hi[:, 0], full[:, :, :], ACT.Copy).then_inc(w_hi, 1)

            def keep_qk(u, j, i):
                h, hg = divmod(u, 2)
                wait(act, qk_done, 2 * u + j + 1, i, 2 * PERIOD)
                if j == 0:
                    per_half(act, q_placed[hg], h - 1, i, 16 * HPG)
                    nc.scalar.activation(q_cut[:, hg, 0].rearrange("p (c r) -> p r c", c=32),
                                         ps_qk[:, :].rearrange("p (r c) -> p r c", c=32), ACT.Copy).then_inc(qk_hi, 1)
                else:
                    per_step(act, scored, 2 * (h - 2) + 1, i)
                    nc.scalar.activation(k_sb[:, h % 2, hg, 0], ps_qk[:, :], ACT.Copy).then_inc(qk_hi, 1)

            def step(t, i):
                if is_step(t - 1):
                    g = t - 1
                    per_step(act, transposed, g, i)
                    per_step(act, pv_done, g - 2, i)
                    nc.scalar.activation(pt[:, g % 2, 0], ps_t[:, :], ACT.Copy).then_inc(pt_hi, 1)
                u = t + PROJ_LEAD
                if is_step(u):
                    keep_qk(u, 0, i)
                h = half_at(t, SPLIT_LEAD)
                if h is not None:
                    per_half(act, normed, h, i)
                    per_half(act, qk_done, h - 2, i, 4)
                    per_step(act, v_done, 2 * (h - 2) + 1, i)
                    nc.scalar.activation(xhi[:, h % 2], xn[:, :, :], ACT.Copy).then_inc(x_hi, 1)
                b = image_at(t, SQ_LEAD)
                if b is not None:
                    wait(act, x_loaded[b % XBUFS], 16 * (b // XBUFS + 1), i, 16)
                    per_image(act, summed_x, b - 1, i, 2)
                    nc.scalar.activation(sq[:, 0, :], x_sb[:, b % XBUFS, 0], ACT.Square).then_inc(squared, 1)
                if is_step(t):
                    per_step(act, shifted, t, i)
                    nc.scalar.activation(sc[:, t % 2], sc[:, t % 2], ACT.Exp).then_inc(exped, 1)
                if is_step(u):
                    per_step(act, v_done, u, i)
                    per_step(act, v_kept, u - 1, i)
                    values = ps_vo[:, :].rearrange("p (t c) -> p t c", t=T2)[:, :, 0:C]
                    nc.scalar.activation(v_f[:, :].rearrange("p (t c) -> p t c", t=T2), values, ACT.Copy).then_inc(v_out, 1)
                    nc.scalar.activation(v_sb[:, u % VBUFS, 0].rearrange("p (t h d) -> p t h d", t=T2, d=DP)[:, :, :, 0:D],
                                         values.rearrange("p t (h d) -> p t h d", d=D), ACT.Copy).then_inc(v_hi, 1)
                b = image_at(t, SQ_LEAD)
                if b is not None:
                    nc.scalar.activation(sq[:, 1, :], x_sb[:, b % XBUFS, 1], ACT.Square).then_inc(squared, 1)
                if is_step(u):
                    keep_qk(u, 1, i)
                if is_step(t - 1):
                    g = t - 1
                    per_step(act, pv_done, g, i)
                    per_step(act, projected, g - 2, i)
                    for hd in range(HPG):
                        p = slice(hd * DP, hd * DP + DP)
                        last = nc.scalar.activation(
                            o_f[p, g % 2].rearrange("p u (pr i) -> p u pr i", i=32),
                            ps_pv[p, :, :].rearrange("p pr (u h i) -> p u pr h i", u=T2 * HG, h=HPG)[:, :, :, hd, :],
                            ACT.Copy)
                    last.then_inc(o_kept, 1)
                    per_step(act, o_kept, g, i)
                    nc.scalar.activation(ohi[:, g % 2], in_x_order(o_f[:, g % 2]), ACT.Copy).then_inc(o_hi, 1)

            rounds(act, step)

        @block.vector
        def _(dve):
            nc.vector.memset(wqk_f[:, :, :], 0.0).then_inc(zeroed, 1)
            nc.vector.memset(x_scale[:, :], X_SCALE).then_inc(zeroed, 1)
            nc.vector.memset(wo_f[:, :, :], 0.0).then_inc(zeroed, 1)
            nc.vector.memset(pos_f[:, :, :], MASK).then_inc(zeroed, 1)
            nc.vector.memset(ones[:, :], 1.0).then_inc(zeroed, 1)
            nc.vector.memset(three_halves[:, :], 1.5).then_inc(zeroed, 1)
            nc.vector.memset(q_bd[:, :, :, :, :, :].rearrange("p a b c d e -> p (a b c d e)").bitcast(F32), 0.0).then_inc(zeroed, 1)
            nc.vector.memset(w_max[:, :], 0.0).then_inc(zeroed, 1)
            dve.wait_ge(zeroed, 8)
            dve.wait_ge(weights_loaded, 16 * N_WEIGHTS)
            for n, w in enumerate((wqk_f[:, :, 0:256], wqk_f[:, :, 256:512], wv_f[:, :, :])):
                nc.vector.tensor_reduce(w_max[0:CP, n:n + 1], w, AX.XY, ALU.max,
                                        apply_absolute_value=True).then_inc(w_absmax, 1)
            dve.wait_ge(w_allmax, 1)
            n_factor = 0

            def factor(ins):
                nonlocal n_factor
                n_factor += 1
                ins.then_inc(w_factor, 1)
                dve.wait_ge(w_factor, n_factor)

            exponent = 0x7F800000
            factor(nc.vector.tensor_scalar(w_top[:, :], w_top[:, :], 2.0 ** -100, None, ALU.max))
            factor(nc.vector.tensor_scalar(w_pow[:, :], w_top[:, :].bitcast(I32), exponent, None, ALU.bitwise_and))
            factor(nc.vector.tensor_scalar(alpha[:, :], w_pow[:, :], -1.0, float((254 - 1) << 23), ALU.mult, ALU.add))
            factor(nc.vector.tensor_scalar(unscale[:, :], w_pow[:, :].bitcast(F32), 0.125, None, ALU.mult))
            factor(nc.vector.tensor_tensor(s_scale[:, :], unscale[:, 0:1], unscale[:, 1:2], ALU.mult))
            factor(nc.vector.tensor_tensor(s_scale[:, :], s_scale[:, :], scale_sb[:, :], ALU.mult))
            factors = alpha[:, :].bitcast(F32)
            for n, (w, parts) in enumerate(((wqk_f[:, :, 0:256], CP), (wqk_f[:, :, 256:512], CP), (wv_f[:, :, :], CP))):
                nc.vector.tensor_scalar(w, w, factors[0:parts, n:n + 1], None, ALU.mult).then_inc(w_scaled, 1)
            nc.vector.tensor_scalar(wo_f[:, :, :], wo_f[:, :, :], unscale[:, 2:3], None, ALU.mult).then_inc(w_scaled, 1)
            dve.wait_ge(w_hi, 3)
            nc.vector.tensor_copy(pos_sb[:, :, :, :], pos_f[:, :, :].unsqueeze(2).broadcast_to((128, HG, PAIRS, 32))).then_inc(pos_ready, 1)
            dve.wait_ge(pos_ready, 1)
            for parts, full in ((wqk, wqk_f), (wv_s, wv_f), (wo_s, wo_f)):
                nc.vector.tensor_tensor(parts[:, 1], full[:, :, :], parts[:, 0], ALU.subtract).then_inc(w_lo, 1)

            def keep_qk(u, j, i):
                h, hg = divmod(u, 2)
                wait(dve, qk_hi, 2 * u + j + 1, i, 2 * PERIOD)
                if j == 0:
                    out_, hi_ = (q_cut[:, hg, a].rearrange("p (c r) -> p r c", c=32) for a in (1, 0))
                    nc.vector.tensor_tensor(out_, ps_qk[:, :].rearrange("p (r c) -> p r c", c=32), hi_,
                                            ALU.subtract).then_inc(qk_kept, 1)
                else:
                    nc.vector.tensor_tensor(k_sb[:, h % 2, hg, 1], ps_qk[:, :], k_sb[:, h % 2, hg, 0],
                                            ALU.subtract).then_inc(qk_kept, 1)

            def stat_op(b, i, n, make):
                wait(dve, stats, STAT_OPS * b + n, i, STAT_OPS * XBUFS)
                make().then_inc(stats, 1)

            def stat_ops(b, i):
                mean, msq = st[:, 0:G], st[:, G:2 * G]
                two = (CP, G, WW // G)
                yield lambda: nc.vector.tensor_scalar(st[:, :], ps_s[0:CP, 0:2 * G], 1.0 / GROUP_N, None, ALU.mult)
                yield lambda: nc.vector.tensor_copy(mean_w[:, :].rearrange("p (g w) -> p g w", g=G),
                                                    mean.unsqueeze(2).broadcast_to(two))
                yield lambda: nc.vector.scalar_tensor_tensor(var[:, :], mean, -1.0, mean, ALU.mult, ALU.mult)
                yield lambda: nc.vector.tensor_tensor(var[:, :], var[:, :], msq, ALU.add)
                yield lambda: nc.vector.tensor_scalar(var[:, :], var[:, :], 0.0, EPS, ALU.max, ALU.add)
                yield lambda: nc.vector.tensor_scalar(half_var[:, :], var[:, :], 0.5, None, ALU.mult)
                yield lambda: nc.vector.tensor_scalar(guess[:, :], var[:, :].bitcast(I32), 1, None, ALU.logical_shift_right)
                yield lambda: nc.vector.tensor_scalar(guess[:, :], guess[:, :], -1.0, float(0x5F3759DF), ALU.mult, ALU.add)

            def step(t, i):
                g = t - FINAL_LAG
                if is_step(g):
                    b = g // 4
                    per_step(dve, projected, g, i)
                    for ch in range(CH):
                        r0 = (g % 4) * T2
                        xr = x_sb[:, b % XBUFS, ch].rearrange("p (nh y) -> p nh y", nh=NW)[:, :, r0 * WW:(r0 + T2) * WW]
                        last = nc.vector.scalar_tensor_tensor(
                            xr, ps_vo[0:CP, ch * 256:ch * 256 + 256].rearrange("p (nh y) -> p nh y", nh=NW),
                            bo_sb[:, ch:ch + 1], xr, ALU.add, ALU.add)
                    last.then_inc(final, 1)
                if is_step(t):
                    per_step(dve, scored, t, i)
                    nc.vector.scalar_tensor_tensor(
                        sc[:, t % 2].rearrange("p (t2 c) -> p t2 c", t2=T2),
                        ps_s[:, :].rearrange("p (t2 c) -> p t2 c", t2=T2), s_scale[:, :],
                        pos_sb[:, :, :, :].rearrange("p hg pr c -> p (hg pr c)").unsqueeze(1).broadcast_to((128, T2, HG * PAIRS * 32)),
                        ALU.mult, ALU.add).then_inc(biased, 1)
                rows = sc[:, t % 2].rearrange("p (u c) -> p u c", c=32)
                if is_step(t):
                    per_step(dve, biased, t, i)
                    nc.vector.reduce_max(mx[:, t % 2], rows, axis=AX.X).then_inc(maxed, 1)
                g = t - 1
                if is_step(g):
                    per_step(dve, pt_hi, g, i)
                    nc.vector.tensor_tensor(pt[:, g % 2, 1], ps_t[:, :], pt[:, g % 2, 0], ALU.subtract).then_inc(pt_kept, 1)
                u = t + PROJ_LEAD
                if is_step(u):
                    keep_qk(u, 0, i)
                h = half_at(t, CENTRE_LEAD)
                if h is not None:
                    b, hh = divmod(h, 2)
                    per_image(dve, stats, b, i, STAT_OPS)
                    if hh == 0:
                        wait(dve, x_loaded[b % XBUFS], 16 * (b // XBUFS + 1), i, 16)
                    per_half(dve, normed, h - 1, i)
                    for ch in range(CH):
                        nc.vector.tensor_tensor(
                            xc[:, ch, :].rearrange("p (r nh w) -> p nh r w", nh=NW, w=WW),
                            x_sb[:, b % XBUFS, ch].rearrange("p (nh r w) -> p nh r w", nh=NW, r=WS)[:, :, hh * 4:hh * 4 + 4, :],
                            mean_w[:, :].unsqueeze(1).unsqueeze(1).broadcast_to((CP, NW, WS // 2, WW)),
                            ALU.subtract).then_inc(centred, 1)
                h = half_at(t, NORM_LEAD)
                if h is not None:
                    per_half(dve, x_hi, h - 1, i)
                    per_half(dve, x_lo, h - 1, i)
                    per_half(dve, centred, h, i, CH)
                    per_image(dve, rstd_ready, h // 2, i)
                    nc.vector.tensor_tensor(
                        xn[:, :, :].rearrange("p ch (r c n) -> p (ch r) c n", c=WS, n=WIN),
                        xc[:, :, :].rearrange("p ch (r n c) -> p (ch r) c n", c=WS, n=WIN),
                        rstd_t[:, :].rearrange("p (c n) -> p c n", n=WIN).unsqueeze(1).broadcast_to((CP, CH * WS // 2, WS, WIN)),
                        ALU.mult).then_inc(normed, 1)
                if is_step(t):
                    per_step(dve, exped, t, i)
                    nc.vector.reduce_sum(sm[:, t % 2], rows, axis=AX.X).then_inc(row_sum, 1)
                    per_step(dve, row_sum, t, i)
                    nc.vector.reciprocal(rs[:, t % 2], sm[:, t % 2]).then_inc(inverted, 1)
                b = image_at(t, STAT_LEAD)
                if b is not None:
                    per_image(dve, totals, b, i)
                    per_half(dve, normed, 2 * b - 1, i)
                    per_image(dve, rstd_ready, b - 1, i)
                    for n, make in enumerate(stat_ops(b, i)):
                        stat_op(b, i, n, make)
                by_group = "p (y g w) -> p g y w"
                b = image_at(t, RSUM_LEAD)
                if b is not None:
                    wait(dve, x_loaded[b % XBUFS], 16 * (b // XBUFS + 1), i, 16)
                    per_image(dve, totals, b - 1, i)
                    nc.vector.tensor_reduce(part[:, 0:G], x_sb[:, b % XBUFS].rearrange("p ch n -> p (ch n)")
                                            .rearrange(by_group, g=G, w=WW // G),
                                            AX.XY, ALU.add).then_inc(summed_x, 1)
                b = image_at(t, RSQ_LEAD)
                if b is not None:
                    per_image(dve, squared, b, i, CH)
                    nc.vector.tensor_reduce(part[:, G:2 * G], sq[:, :, :].rearrange("p ch n -> p (ch n)")
                                            .rearrange(by_group, g=G, w=WW // G),
                                            AX.XY, ALU.add).then_inc(summed_x, 1)
                if is_step(u):
                    keep_qk(u, 1, i)

            rounds(dve, step)

        @block.gpsimd
        def _(pool):
            nc.gpsimd.memset(ident[:, :], 0.0).then_inc(ident_zero, 1)
            nc.gpsimd.memset(v_sb[:, :, :, :].rearrange("p a b c -> p (a b c)").bitcast(F32), 0.0).then_inc(v_zeroed, 1)
            pool.wait_ge(ident_zero, 1)
            nc.gpsimd.affine_select(out=ident[:, :], in_=ident[:, :], compare_op=ALU.not_equal, fill=1.0,
                                    base=0, pattern=[[-1, 128]], channel_multiplier=1).then_inc(ident_ready, 1)

            def root(b, i):
                per_image(pool, stats, b, i, STAT_OPS)
                per_half(pool, normed, 2 * b - 1, i)
                n = 0
                y = guess[:, :].bitcast(F32)
                for k in range(NEWTON):
                    for make in (lambda: nc.gpsimd.tensor_tensor(newton[:, :], y, y, ALU.mult),
                                 lambda: nc.gpsimd.tensor_tensor(newton[:, :], newton[:, :], half_var[:, :], ALU.mult),
                                 lambda: nc.gpsimd.tensor_tensor(newton[:, :], three_halves[:, :], newton[:, :], ALU.subtract),
                                 lambda: nc.gpsimd.tensor_tensor(rstd[:, :], y, newton[:, :], ALU.mult)):
                        wait(pool, refined, ROOT_OPS * b + n, i, ROOT_OPS * XBUFS)
                        make().then_inc(refined, 1)
                        n += 1
                    y = rstd[:, :]
                per_image(pool, refined, b, i, ROOT_OPS)
                c2 = WS // 2
                by_token = (CP, c2, 2 * NW, NW)
                nc.gpsimd.tensor_tensor(
                    rstd_t[:, :].rearrange("p (c x nw) -> p c x nw", c=c2, nw=NW),
                    rstd[:, :].rearrange("p (nw c) -> p c nw", c=c2).unsqueeze(2).broadcast_to(by_token),
                    x_scale[:, :].unsqueeze(1).unsqueeze(1).broadcast_to(by_token), ALU.mult).then_inc(rstd_ready, 1)

            def step(t, i):
                rows = sc[:, t % 2].rearrange("p (u c) -> p u c", c=32)
                by_row = (128, UNIT, 32)
                if is_step(t):
                    per_step(pool, maxed, t, i)
                    nc.gpsimd.tensor_tensor(rows, rows, mx[:, t % 2].unsqueeze(2).broadcast_to(by_row),
                                            ALU.subtract).then_inc(shifted, 1)
                g = t - OUT_LAG
                if is_step(g):
                    per_step(pool, o_hi, g, i)
                    nc.gpsimd.tensor_tensor(olo[:, g % 2], in_x_order(o_f[:, g % 2]), ohi[:, g % 2],
                                            ALU.subtract).then_inc(o_lo, 1)
                u = t + PROJ_LEAD
                if is_step(u):
                    per_step(pool, v_hi, u, i)
                    rest, lead = (v_sb[:, u % VBUFS, a].rearrange("p (h d) -> p h d", d=DP)[:, :, 0:D] for a in (1, 0))
                    nc.gpsimd.tensor_tensor(rest, v_f[:, :].rearrange("p (h d) -> p h d", d=D), lead,
                                            ALU.subtract).then_inc(v_kept, 1)
                if is_step(t):
                    per_step(pool, inverted, t, i)
                    nc.gpsimd.tensor_tensor(rows, rows, rs[:, t % 2].unsqueeze(2).broadcast_to(by_row),
                                            ALU.mult).then_inc(probs, 1)
                b = image_at(t, STAT_LEAD)
                if b is not None:
                    root(b, i)
                h = half_at(t, SPLIT_LEAD)
                if h is not None:
                    per_half(pool, x_hi, h, i)
                    nc.gpsimd.tensor_tensor(xlo[:, h % 2], xn[:, :, :], xhi[:, h % 2],
                                            ALU.subtract).then_inc(x_lo, 1)

            pool.wait_ge(zeroed, 8)
            pool.wait_ge(w_absmax, 3)
            nc.gpsimd.partition_all_reduce(w_top[:, :], w_max[:, :], 128, bass.bass_isa.ReduceOp.max).then_inc(w_allmax, 1)
            rounds(pool, step)


N_WEIGHTS = 2 * CH + CH + HG * (HPG + 2 * HPG) + 2

_INS = ["x", "L0_conv_Wq", "L0_conv_Wk", "L0_conv_Wv", "L0_conv_Wo", "L0_conv_bo", "L0_conv_pos_emb", "L0_conv_scale"]


def kernel(**inputs):
    import numpy as np
    import concourse.bacc as bacc
    from concourse.bass_utils import run_bass_kernel_spmd

    nc = bacc.Bacc("TRN2", target_bir_lowering=False, num_devices=1)
    arrays, args = {}, []
    for name in _INS:
        a = np.ascontiguousarray(inputs[name])
        arrays[f"in_{name}"] = a
        args.append(nc.dram_tensor(f"in_{name}", a.shape, F32, kind="ExternalInput").ap())
    out = nc.dram_tensor("out_y", (B, C, HH, WW), F32, kind="ExternalOutput").ap()
    build(nc, *args, out)
    r = run_bass_kernel_spmd(nc, [arrays], core_ids=[0])
    return r.results[0]["out_y"]
```

```python
from contextlib import ExitStack

import concourse.bass as bass
from concourse import mybir
from concourse.alu_op_type import AluOpType as ALU

ACT = mybir.ActivationFunctionType
AX = mybir.AxisListType
F32 = mybir.dt.float32
F32R = mybir.dt.float32r
I32 = mybir.dt.int32
F16 = mybir.dt.float16

B, C, HH, WW = 128, 224, 32, 32
WS = 8
NW = HH // WS
TOK = HH * WW
CH, CP = 2, C // 2
HEADS = 8
D = C // HEADS
DP = 32
HG = 2
HPG = HEADS // HG
WIN = NW * NW
PAIRS = 4
TILE = 128
T2 = 2
STEPS = B * TOK // (T2 * TILE)
HALVES = STEPS // 2
HTOK = TOK // 2
G = 16
GROUP_N = C * HH * (WW // G)
EPS = 1e-5
MASK = -1e30
X_SCALE = 16.0
PASSES = ((0, 0), (0, 1), (1, 0))
UNIT = T2 * HG * PAIRS
XBUFS = 4
VT = 2 * T2 * HG

LOAD_LEAD, RSUM_LEAD, SQ_LEAD, RSQ_LEAD, STAT_LEAD = 10, 9, 9, 8, 7
CENTRE_LEAD, NORM_LEAD, SPLIT_LEAD, PROJ_LEAD, PLACE_LEAD = 6, 5, 4, 3, 1
OUT_LAG, FINAL_LAG, STORE_LAG = 2, 3, 6
PERIOD = 4 * XBUFS
FIRST = -LOAD_LEAD
LOOP_AT = 4
ROUNDS = (STEPS - LOAD_LEAD - LOOP_AT) // PERIOD
LOOP_END = LOOP_AT + ROUNDS * PERIOD
LAST = STEPS + STORE_LAG - 2


def build(nc, x, wq, wk, wv, wo, bo, pos, scale, out):
    ctx = ExitStack()
    with ctx:
        def sb(name, shape, dt=F32):
            return ctx.enter_context(nc.sbuf_tensor(name, shape, dt))

        def sem(name):
            return ctx.enter_context(nc.semaphore(name))

        x_sb = sb("x_sb", [CP, XBUFS, CH, TOK])
        sq = sb("sq", [CP, CH, TOK])
        part = sb("part", [CP, CH, 2 * G])
        st = sb("st", [CP, 2 * G])
        var = sb("var", [CP, G])
        mean_w = sb("mean_w", [CP, WW])
        guess = sb("guess", [CP, G], I32)
        rstd = sb("rstd", [CP, G])
        half_var = sb("half_var", [CP, G])
        three_halves = sb("three_halves", [CP, G])
        newton = sb("newton", [CP, G])
        rstd_t = sb("rstd_t", [CP, TILE])
        xc = sb("xc", [CP, CH, HTOK])
        xn = sb("xn", [CP, CH, HTOK])
        xhi = sb("xhi", [CP, 2, CH, HTOK], F16)
        xlo = sb("xlo", [CP, 2, CH, HTOK], F16)
        q_cut = sb("q_cut", [128, HG, 2, HTOK], F16)
        q_bd = sb("q_bd", [128, 2, HG, 2, HPG, HTOK], F16)
        k_sb = sb("k_sb", [128, 2, HG, 2, HTOK], F16)
        v_f = sb("v_f", [128, HPG * D, T2 * HG])
        v_cut = sb("v_cut", [128, 2, 2, HPG * D, VT], F16)
        v_bd = sb("v_bd", [128, 2, 2, PAIRS, 128, VT], F16)
        sc = sb("sc", [128, 2, UNIT * 32])
        mx = sb("mx", [128, 2, UNIT])
        sm = sb("sm", [128, 2, UNIT])
        rs = sb("rs", [128, 2, UNIT])
        pt_f = sb("pt_f", [128, UNIT * 32])
        pt = sb("pt", [128, 2, 2, UNIT * 32], F16)
        o_f = sb("o_f", [128, 2, T2 * HG, WIN, WS])
        ohi = sb("ohi", [128, 2, T2 * HG, WIN, WS], F32R)
        olo = sb("olo", [128, 2, T2 * HG, WIN, WS], F32R)
        wqk_f = sb("wqk_f", [CP, CH, 2 * 256])
        wqk = sb("wqk", [CP, 2, CH, 2 * 256], F16)
        wv_f = sb("wv_f", [CP, CH, C])
        wv_s = sb("wv_s", [CP, 2, CH, C], F16)
        wo_f = sb("wo_f", [128, HG, C])
        wo_s = sb("wo_s", [128, 2, HG, C], F32R)
        bo_sb = sb("bo_sb", [CP, CH])
        scale_sb = sb("scale_sb", [128, 1])
        w_max = sb("w_max", [128, 3])
        w_top = sb("w_top", [128, 3])
        w_pow = sb("w_pow", [128, 3], I32)
        alpha = sb("alpha", [128, 3], I32)
        unscale = sb("unscale", [128, 3])
        s_scale = sb("s_scale", [128, 1])
        pos_f = sb("pos_f", [128, HG, 32])
        pos_sb = sb("pos_sb", [128, HG, PAIRS, 32])
        ones = sb("ones", [CP, CP])
        x_scale = sb("x_scale", [CP, 1])

        ps_q = ctx.enter_context(nc.psum_tensor("ps_q", [128, HTOK], F32))
        ps_k = ctx.enter_context(nc.psum_tensor("ps_k", [128, HTOK], F32))
        ps_qk = (ps_q, ps_k)
        ps_v = ctx.enter_context(nc.psum_tensor("ps_v", [128, T2, 256], F32))
        ps_out = ctx.enter_context(nc.psum_tensor("ps_out", [128, 512], F32))
        ps_s = [ctx.enter_context(nc.psum_tensor(f"ps_s{n}", [128, UNIT * 32], F32)) for n in range(2)]
        ps_o = ctx.enter_context(nc.psum_tensor("ps_o", [128, UNIT * 32], F32))
        ps_tot = ctx.enter_context(nc.psum_tensor("ps_tot", [128, 2 * G], F32))

        x_loaded = [sem(f"x_loaded{s}") for s in range(XBUFS)]
        y_stored = [sem(f"y_stored{s}") for s in range(XBUFS)]
        weights_loaded = sem("weights_loaded")
        zeroed = sem("zeroed")
        pos_ready = sem("pos_ready")
        v_zeroed = sem("v_zeroed")
        w_absmax = sem("w_absmax")
        w_allmax = sem("w_allmax")
        w_factor = sem("w_factor")
        w_scaled = sem("w_scaled")
        w_hi = sem("w_hi")
        w_lo = sem("w_lo")
        summed_x = sem("summed_x")
        squared = sem("squared")
        totals = sem("totals")
        stats = sem("stats")
        refined = sem("refined")
        rstd_ready = sem("rstd_ready")
        centred = sem("centred")
        normed = sem("normed")
        x_hi = sem("x_hi")
        x_lo = sem("x_lo")
        qk_done = sem("qk_done")
        qk_hi = sem("qk_hi")
        qk_kept = sem("qk_kept")
        q_placed = sem("q_placed")
        v_placed = [sem(f"v_placed{n}") for n in range(2)]
        v_done = sem("v_done")
        v_out = sem("v_out")
        v_hi = sem("v_hi")
        v_kept = sem("v_kept")
        scored = sem("scored")
        biased = sem("biased")
        maxed = sem("maxed")
        shifted = sem("shifted")
        exped = sem("exped")
        row_sum = sem("row_sum")
        inverted = sem("inverted")
        probs = sem("probs")
        turned = sem("turned")
        pt_hi = sem("pt_hi")
        pt_kept = sem("pt_kept")
        pv_done = sem("pv_done")
        o_kept = sem("o_kept")
        o_hi = sem("o_hi")
        o_lo = sem("o_lo")
        projected = sem("projected")
        final = sem("final")
        STAT_OPS = 8
        NEWTON = 3
        ROOT_OPS = 4 * NEWTON

        def wait(eng, s, n, i, per_round):
            if isinstance(i, int):
                if n > 0:
                    eng.wait_ge(s, n)
            else:
                assert n > 0
                eng.wait_ge(s, n + i * per_round)

        def rounds(eng, step):
            for t in range(FIRST, LOOP_AT):
                step(t, 0)
            with eng.Fori(0, ROUNDS) as i:
                for t in range(LOOP_AT, LOOP_AT + PERIOD):
                    step(t, i)
            for t in range(LOOP_END, LAST + 1):
                step(t, 0)

        def per_step(eng, s, g, i, each=1):
            wait(eng, s, each * (g + 1), i, each * PERIOD)

        def per_half(eng, s, h, i, each=1):
            wait(eng, s, each * (h + 1), i, each * PERIOD // 2)

        def per_image(eng, s, b, i, each=1):
            wait(eng, s, each * (b + 1), i, each * PERIOD // 4)

        def values_placed(eng, h, i):
            each = 16 * HPG * PAIRS
            wait(eng, v_placed[h % 2], each * (h // 2 + 1), i, each * PERIOD // 4)

        def image_at(t, lead):
            b, r = divmod(t + lead, 4)
            return b if r == 0 and 0 <= b < B else None

        def half_at(t, lead):
            h, r = divmod(t + lead, 2)
            return h if r == 0 and 0 <= h < HALVES else None

        def is_step(g):
            return 0 <= g < STEPS

        def in_x_order(ap):
            return ap.rearrange("p u (c n) -> p u n c", c=WS)

        def cut_values(u, part):
            n = (u % 2) * T2 * HG
            return v_cut[:, (u // 2) % 2, part, :, n:n + T2 * HG]

        def centre(engine, h, i):
            b, hh = divmod(h, 2)
            for ch in range(CH):
                engine.tensor_tensor(
                    xc[:, ch, :].rearrange("p (r nh w) -> p nh r w", nh=NW, w=WW),
                    x_sb[:, b % XBUFS, ch].rearrange("p (nh r w) -> p nh r w", nh=NW, r=WS)[:, :, hh * 4:hh * 4 + 4, :],
                    mean_w[:, :].unsqueeze(1).unsqueeze(1).broadcast_to((CP, NW, WS // 2, WW)),
                    ALU.subtract).then_inc(centred, 1)

        block = ctx.enter_context(nc.Block())

        @block.sync
        def _(sp):
            sp.wait_ge(zeroed, 8)
            n_w = 0

            def load_weights(dst, src):
                sp.dma_start(dst, src).then_inc(weights_loaded, 16)

            for kind, w in ((0, wq), (1, wk)):
                for ch in range(CH):
                    load_weights(wqk_f[:, ch, kind * 256:kind * 256 + 256].rearrange("p (h d) -> p h d", d=DP)[:, :, 0:D],
                                 w[ch * CP:(ch + 1) * CP, :].rearrange("p (h d) -> p h d", d=D))
                    n_w += 1
            for ch in range(CH):
                load_weights(wv_f[:, ch, :], wv[ch * CP:(ch + 1) * CP, :])
                n_w += 1
            for hg in range(HG):
                for h in range(HPG):
                    row = (hg * HPG + h) * D
                    load_weights(wo_f[h * DP:h * DP + D, hg, :], wo[row:row + D, :])
                    n_w += 1
                for h in range(HPG):
                    for a in range(2):
                        p0 = h * 32 + a * WIN
                        load_weights(pos_f[p0:p0 + WIN, hg, a * WIN:(a + 1) * WIN], pos[0, 0, hg * HPG + h])
                        n_w += 1
            sp.dma_start(bo_sb[:, :], bo.rearrange("(ch p) -> p ch", p=CP),
                         allow_slow_non_contiguous=True).then_inc(weights_loaded, 16)
            load_weights(scale_sb[:, :], scale.partition_broadcast(128))
            assert n_w + 2 == N_WEIGHTS

            def step(t, i):
                g = t + PLACE_LEAD
                if is_step(g):
                    h, hh = divmod(g, 2)
                    per_step(sp, v_kept, 2 * h + 1, i)
                    for pr in (2 * hh, 2 * hh + 1):
                        for hd in range(HPG):
                            sp.dma_start(v_bd[hd * 32:hd * 32 + 32, h % 2, :, pr, hd * DP:hd * DP + D, :],
                                         v_cut[pr * 32:pr * 32 + 32, h % 2, :, hd * D:hd * D + D, :]).then_inc(v_placed[h % 2], 16)
                b = image_at(t, -STORE_LAG)
                if b is not None:
                    per_step(sp, final, 4 * b + 3, i, CH)
                    sp.dma_start(out[b + i * XBUFS].rearrange("(ch p) y z -> p ch (y z)", p=CP) if isinstance(i, int)
                                 else out[bass.ds(b + i * XBUFS, 1)].rearrange("o (ch p) y z -> p (o ch) (y z)", p=CP),
                                 x_sb[:, b % XBUFS]).then_inc(y_stored[b % XBUFS], 16)
                u = t + PROJ_LEAD
                if is_step(u) and u % 2 == 1:
                    h = u // 2
                    wait(sp, qk_kept, 2 * u + 1, i, 2 * PERIOD)
                    for hd in range(HPG):
                        p = slice(hd * DP, hd * DP + DP)
                        sp.dma_start(q_bd[p, h % 2, :, :, hd, :], q_cut[p]).then_inc(q_placed, 16)
                b = image_at(t, LOAD_LEAD)
                if b is not None:
                    wait(sp, y_stored[b % XBUFS], 16 * (b // XBUFS), i, 16)
                    sp.dma_start(x_sb[:, b % XBUFS],
                                 x[b + i * XBUFS].rearrange("(ch p) y z -> p ch (y z)", p=CP) if isinstance(i, int)
                                 else x[bass.ds(b + i * XBUFS, 1)].rearrange("o (ch p) y z -> p (o ch) (y z)", p=CP)
                                 ).then_inc(x_loaded[b % XBUFS], 16)

            rounds(sp, step)
            for s in range(XBUFS):
                sp.wait_ge(y_stored[s], 16 * (B // XBUFS))

        @block.tensor
        def _(pe):
            def split_product(dst, w_parts, x_parts, chunks):
                n = 0
                for a, c in PASSES:
                    for ch in range(chunks):
                        last = nc.tensor.matmul(dst, w_parts(a, ch), x_parts(c, ch),
                                                start=(n == 0), stop=(n == 3 * chunks - 1))
                        n += 1
                return last

            x_parts = (xhi, xlo)
            o_parts = (ohi, olo)

            def project_qk(u, j, i):
                h, hg = divmod(u, 2)
                if hg == 0 and j == 0:
                    per_half(pe, x_hi, h, i)
                    per_half(pe, x_lo, h, i)
                wait(pe, qk_kept, 2 * (u - 1) + j + 1, i, 2 * PERIOD)
                c0 = (j * HG + hg) * 128
                split_product(ps_qk[j][:, :], lambda a, ch: wqk[:, a, ch, c0:c0 + 128],
                              lambda c, ch: x_parts[c][:, h % 2, ch, :], CH).then_inc(qk_done, 1)

            def project_v(g, i):
                h = g // 2
                per_step(pe, v_hi, g - 1, i)
                for t2 in range(T2):
                    tok = (g % 2) * 256 + t2 * TILE
                    last = split_product(ps_v[:, t2, 0:C],
                                         lambda a, ch: x_parts[a][:, h % 2, ch, tok:tok + TILE],
                                         lambda c, ch: wv_s[:, c, ch, :], CH)
                last.then_inc(v_done, 1)

            def score(g):
                for t2 in range(T2):
                    for hg in range(HG):
                        for pr in range(PAIRS):
                            pair = ((g % 2) * T2 + t2) * PAIRS + pr
                            col = ((t2 * HG + hg) * PAIRS + pr) * 32
                            for n, (a, c) in enumerate(PASSES):
                                last = nc.tensor.matmul(
                                    ps_s[g % 2][:, col:col + 32],
                                    q_bd[:, (g // 2) % 2, hg, a].rearrange("p h (c r) -> p (h c) r", r=HTOK // 32)[:, :, pair],
                                    k_sb[:, (g // 2) % 2, hg, c, pair * 32:pair * 32 + 32],
                                    start=(n == 0), stop=(n == 2))
                return last

            def weigh_values(g):
                for t2 in range(T2):
                    for hg in range(HG):
                        for pr in range(PAIRS):
                            col = ((t2 * HG + hg) * PAIRS + pr) * 32
                            for n, (a, c) in enumerate(PASSES):
                                last = nc.tensor.matmul(
                                    ps_o[:, col:col + 32],
                                    v_bd[:, (g // 2) % 2, a, pr, :, ((g % 2) * T2 + t2) * HG + hg],
                                    pt[:, g % 2, c, col:col + 32],
                                    start=(n == 0), stop=(n == 2))
                return last

            def step(t, i):
                u = t + PROJ_LEAD
                if is_step(u):
                    project_qk(u, 0, i)
                    project_v(u, i)
                    project_qk(u, 1, i)
                g = t + 1
                if is_step(g):
                    if g % 2 == 0:
                        per_half(pe, q_placed, g // 2, i, 16 * HPG)
                        per_half(pe, qk_kept, g // 2, i, 4)
                    per_step(pe, biased, g - 2, i)
                    score(g).then_inc(scored, 1)
                if is_step(t - 1):
                    g = t - 1
                    per_step(pe, pt_kept, g, i)
                    if g % 2 == 0:
                        values_placed(pe, g // 2, i)
                    per_step(pe, o_kept, g - 1, i)
                    per_step(pe, o_hi, g - 1, i)
                    weigh_values(g).then_inc(pv_done, 1)
                b = image_at(t, STAT_LEAD)
                if b is not None:
                    per_image(pe, summed_x, b, i, 2 * CH)
                    wait(pe, stats, STAT_OPS * (b - 1) + 1, i, STAT_OPS * XBUFS)
                    for ch in range(CH):
                        last = nc.tensor.matmul(ps_tot[0:CP, :], ones[:, :], part[:, ch],
                                                start=(ch == 0), stop=(ch == CH - 1))
                    last.then_inc(totals, 1)
                g = t - OUT_LAG
                if is_step(g):
                    per_step(pe, o_hi, g, i)
                    per_step(pe, o_lo, g, i)
                    per_step(pe, final, g - 1, i, CH)
                    for ch in range(CH):
                        last = split_product(ps_out[0:CP, ch * 256:ch * 256 + 256],
                                             lambda a, hg: wo_s[:, a, hg, ch * CP:(ch + 1) * CP],
                                             lambda c, hg: o_parts[c][:, g % 2, hg::HG].rearrange("p t (nh nw) c -> p nh t (nw c)", nh=NW), HG)
                    last.then_inc(projected, 1)

            pe.wait_ge(v_zeroed, 1)
            pe.wait_ge(zeroed, 8)
            pe.wait_ge(w_hi, 3)
            pe.wait_ge(w_lo, 3)
            rounds(pe, step)

        @block.scalar
        def _(act):
            act.wait_ge(w_scaled, 4)
            for hi, full in ((wqk, wqk_f), (wv_s, wv_f), (wo_s, wo_f)):
                nc.scalar.activation(hi[:, 0], full[:, :, :], ACT.Copy).then_inc(w_hi, 1)

            def keep_qk(u, j, i):
                h, hg = divmod(u, 2)
                wait(act, qk_done, 2 * u + j + 1, i, 2 * PERIOD)
                if j == 0:
                    per_half(act, q_placed, h - 1, i, 16 * HPG)
                    nc.scalar.activation(q_cut[:, hg, 0].rearrange("p (c r) -> p r c", c=32),
                                         ps_q[:, :].rearrange("p (r c) -> p r c", c=32), ACT.Copy).then_inc(qk_hi, 1)
                else:
                    per_step(act, scored, 2 * (h - 2) + 1, i)
                    nc.scalar.activation(k_sb[:, h % 2, hg, 0], ps_k[:, :], ACT.Copy).then_inc(qk_hi, 1)

            def step(t, i):
                h = half_at(t, SPLIT_LEAD)
                if h is not None:
                    per_half(act, normed, h, i)
                    per_half(act, qk_done, h - 2, i, 4)
                    per_step(act, v_done, 2 * (h - 2) + 1, i)
                    nc.scalar.activation(xhi[:, h % 2], xn[:, :, :], ACT.Copy).then_inc(x_hi, 1)
                u = t + PROJ_LEAD
                if is_step(u):
                    keep_qk(u, 0, i)
                if is_step(t - 1):
                    per_step(act, turned, t - 1, i)
                    per_step(act, pv_done, t - 3, i)
                    nc.scalar.activation(pt[:, (t - 1) % 2, 0], pt_f[:, :], ACT.Copy).then_inc(pt_hi, 1)
                if is_step(t):
                    per_step(act, shifted, t, i)
                    nc.scalar.activation(sc[:, t % 2], sc[:, t % 2], ACT.Exp).then_inc(exped, 1)
                b = image_at(t, SQ_LEAD)
                if b is not None:
                    wait(act, x_loaded[b % XBUFS], 16 * (b // XBUFS + 1), i, 16)
                    per_image(act, summed_x, b - 1, i, 2 * CH)
                    nc.scalar.activation(sq[:, 0, :], x_sb[:, b % XBUFS, 0], ACT.Square).then_inc(squared, 1)
                if is_step(u):
                    per_step(act, v_done, u, i)
                    per_step(act, v_kept, u - 1, i)
                    h = u // 2
                    values_placed(act, h - 2, i)
                    values = ps_v[:, :, 0:C].rearrange("p t (g x) -> p x t g", g=HG)
                    nc.scalar.activation(v_f[:, :, :].rearrange("p x (t g) -> p x t g", g=HG), values, ACT.Copy).then_inc(v_out, 1)
                    nc.scalar.activation(cut_values(u, 0).rearrange("p x (t g) -> p x t g", g=HG), values, ACT.Copy).then_inc(v_hi, 1)
                b = image_at(t, SQ_LEAD)
                if b is not None:
                    nc.scalar.activation(sq[:, 1, :], x_sb[:, b % XBUFS, 1], ACT.Square).then_inc(squared, 1)
                if is_step(u):
                    keep_qk(u, 1, i)
                if is_step(t - 1):
                    g = t - 1
                    per_step(act, pv_done, g, i)
                    per_step(act, projected, g - 2, i)
                    product = in_x_order(ps_o[:, :].rearrange("p (u n) -> p u n", u=T2 * HG))
                    nc.scalar.activation(o_f[:, g % 2], product, ACT.Copy).then_inc(o_kept, 1)
                    nc.scalar.activation(ohi[:, g % 2], product, ACT.Copy).then_inc(o_hi, 1)

            rounds(act, step)

        @block.vector
        def _(dve):
            nc.vector.memset(wqk_f[:, :, :], 0.0).then_inc(zeroed, 1)
            nc.vector.memset(x_scale[:, :], X_SCALE).then_inc(zeroed, 1)
            nc.vector.memset(wo_f[:, :, :], 0.0).then_inc(zeroed, 1)
            nc.vector.memset(pos_f[:, :, :], MASK).then_inc(zeroed, 1)
            nc.vector.memset(ones[:, :], 1.0).then_inc(zeroed, 1)
            nc.vector.memset(three_halves[:, :], 1.5).then_inc(zeroed, 1)
            nc.vector.memset(q_bd[:, :, :, :, :, :].rearrange("p a b c d e -> p (a b c d e)").bitcast(F32), 0.0).then_inc(zeroed, 1)
            nc.vector.memset(w_max[:, :], 0.0).then_inc(zeroed, 1)
            dve.wait_ge(zeroed, 8)
            dve.wait_ge(weights_loaded, 16 * N_WEIGHTS)
            for n, w in enumerate((wqk_f[:, :, 0:256], wqk_f[:, :, 256:512], wv_f[:, :, :])):
                nc.vector.tensor_reduce(w_max[0:CP, n:n + 1], w, AX.XY, ALU.max,
                                        apply_absolute_value=True).then_inc(w_absmax, 1)
            dve.wait_ge(w_allmax, 1)
            n_factor = 0

            def factor(ins):
                nonlocal n_factor
                n_factor += 1
                ins.then_inc(w_factor, 1)
                dve.wait_ge(w_factor, n_factor)

            exponent = 0x7F800000
            factor(nc.vector.tensor_scalar(w_top[:, :], w_top[:, :], 2.0 ** -100, None, ALU.max))
            factor(nc.vector.tensor_scalar(w_pow[:, :], w_top[:, :].bitcast(I32), exponent, None, ALU.bitwise_and))
            factor(nc.vector.tensor_scalar(alpha[:, :], w_pow[:, :], -1.0, float((254 - 1) << 23), ALU.mult, ALU.add))
            factor(nc.vector.tensor_scalar(unscale[:, :], w_pow[:, :].bitcast(F32), 0.125, None, ALU.mult))
            factor(nc.vector.tensor_tensor(s_scale[:, :], unscale[:, 0:1], unscale[:, 1:2], ALU.mult))
            factor(nc.vector.tensor_tensor(s_scale[:, :], s_scale[:, :], scale_sb[:, :], ALU.mult))
            factors = alpha[:, :].bitcast(F32)
            for n, (w, parts) in enumerate(((wqk_f[:, :, 0:256], CP), (wqk_f[:, :, 256:512], CP), (wv_f[:, :, :], CP))):
                nc.vector.tensor_scalar(w, w, factors[0:parts, n:n + 1], None, ALU.mult).then_inc(w_scaled, 1)
            nc.vector.tensor_scalar(wo_f[:, :, :], wo_f[:, :, :], unscale[:, 2:3], None, ALU.mult).then_inc(w_scaled, 1)
            dve.wait_ge(w_hi, 3)
            nc.vector.tensor_copy(pos_sb[:, :, :, :], pos_f[:, :, :].unsqueeze(2).broadcast_to((128, HG, PAIRS, 32))).then_inc(pos_ready, 1)
            dve.wait_ge(pos_ready, 1)
            for parts, full in ((wqk, wqk_f), (wv_s, wv_f), (wo_s, wo_f)):
                nc.vector.tensor_tensor(parts[:, 1], full[:, :, :], parts[:, 0], ALU.subtract).then_inc(w_lo, 1)

            def keep_qk(u, j, i):
                h, hg = divmod(u, 2)
                wait(dve, qk_hi, 2 * u + j + 1, i, 2 * PERIOD)
                if j == 0:
                    out_, hi_ = (q_cut[:, hg, a].rearrange("p (c r) -> p r c", c=32) for a in (1, 0))
                    nc.vector.tensor_tensor(out_, ps_q[:, :].rearrange("p (r c) -> p r c", c=32), hi_,
                                            ALU.subtract).then_inc(qk_kept, 1)
                else:
                    nc.vector.tensor_tensor(k_sb[:, h % 2, hg, 1], ps_k[:, :], k_sb[:, h % 2, hg, 0],
                                            ALU.subtract).then_inc(qk_kept, 1)

            def stat_ops(b, i):
                mean, msq = st[:, 0:G], st[:, G:2 * G]
                two = (CP, G, WW // G)
                yield lambda: nc.vector.tensor_scalar(st[:, :], ps_tot[0:CP, :], 1.0 / GROUP_N, None, ALU.mult)
                yield lambda: nc.vector.tensor_copy(mean_w[:, :].rearrange("p (g w) -> p g w", g=G),
                                                    mean.unsqueeze(2).broadcast_to(two))
                yield lambda: nc.vector.scalar_tensor_tensor(var[:, :], mean, -1.0, mean, ALU.mult, ALU.mult)
                yield lambda: nc.vector.tensor_tensor(var[:, :], var[:, :], msq, ALU.add)
                yield lambda: nc.vector.tensor_scalar(var[:, :], var[:, :], 0.0, EPS, ALU.max, ALU.add)
                yield lambda: nc.vector.tensor_scalar(half_var[:, :], var[:, :], 0.5, None, ALU.mult)
                yield lambda: nc.vector.tensor_scalar(guess[:, :], var[:, :].bitcast(I32), 1, None, ALU.logical_shift_right)
                yield lambda: nc.vector.tensor_scalar(guess[:, :], guess[:, :], -1.0, float(0x5F3759DF), ALU.mult, ALU.add)

            def small_op(b, n, i):
                if b is None:
                    return
                if n == 0:
                    per_image(dve, totals, b, i)
                    per_half(dve, centred, 2 * b - 1, i, CH)
                    per_image(dve, rstd_ready, b - 1, i)
                wait(dve, stats, STAT_OPS * b + n, i, STAT_OPS * XBUFS)
                list(stat_ops(b, i))[n]().then_inc(stats, 1)

            def normalize(h, i):
                per_half(dve, x_hi, h - 1, i)
                per_half(dve, x_lo, h - 1, i)
                per_half(dve, centred, h, i, CH)
                per_image(dve, rstd_ready, h // 2, i)
                nc.vector.tensor_tensor(
                    xn[:, :, :].rearrange("p ch (r c n) -> p (ch r) c n", c=WS, n=WIN),
                    xc[:, :, :].rearrange("p ch (r n c) -> p (ch r) c n", c=WS, n=WIN),
                    rstd_t[:, :].rearrange("p (c n) -> p c n", n=WIN).unsqueeze(1).broadcast_to((CP, CH * WS // 2, WS, WIN)),
                    ALU.mult).then_inc(normed, 1)

            def add_out(g, ch, i):
                if not is_step(g):
                    return
                b = g // 4
                if ch == 0:
                    per_step(dve, projected, g, i)
                r0 = (g % 4) * T2
                xr = x_sb[:, b % XBUFS, ch].rearrange("p (nh y) -> p nh y", nh=NW)[:, :, r0 * WW:(r0 + T2) * WW]
                nc.vector.scalar_tensor_tensor(
                    xr, ps_out[0:CP, ch * 256:ch * 256 + 256].rearrange("p (nh y) -> p nh y", nh=NW),
                    bo_sb[:, ch:ch + 1], xr, ALU.add, ALU.add).then_inc(final, 1)

            by_group = "p (y g w) -> p g y w"

            def group_sums(b, ch, i):
                if b is None:
                    return
                if ch == 0:
                    wait(dve, x_loaded[b % XBUFS], 16 * (b // XBUFS + 1), i, 16)
                    per_image(dve, totals, b - 1, i)
                nc.vector.tensor_reduce(part[:, ch, 0:G], x_sb[:, b % XBUFS, ch].rearrange(by_group, g=G, w=WW // G),
                                        AX.XY, ALU.add).then_inc(summed_x, 1)

            def group_squares(b, ch, i):
                if b is None:
                    return
                wait(dve, squared, CH * b + ch + 1, i, CH * XBUFS)
                nc.vector.tensor_reduce(part[:, ch, G:2 * G], sq[:, ch].rearrange(by_group, g=G, w=WW // G),
                                        AX.XY, ALU.add).then_inc(summed_x, 1)

            def step(t, i):
                rows = sc[:, t % 2].rearrange("p (u c) -> p u c", c=32)
                small_op(image_at(t, STAT_LEAD - 1), 2, i)
                if is_step(t):
                    per_step(dve, scored, t, i)
                    per_step(dve, turned, t - 2, i)
                    nc.vector.scalar_tensor_tensor(
                        sc[:, t % 2].rearrange("p (t2 c) -> p t2 c", t2=T2),
                        ps_s[t % 2][:, :].rearrange("p (t2 c) -> p t2 c", t2=T2), s_scale[:, :],
                        pos_sb[:, :, :, :].rearrange("p hg pr c -> p (hg pr c)").unsqueeze(1).broadcast_to((128, T2, HG * PAIRS * 32)),
                        ALU.mult, ALU.add).then_inc(biased, 1)
                small_op(image_at(t, STAT_LEAD - 1), 3, i)
                if is_step(t):
                    per_step(dve, biased, t, i)
                    nc.vector.reduce_max(mx[:, t % 2], rows, axis=AX.X).then_inc(maxed, 1)
                small_op(image_at(t, STAT_LEAD - 1), 4, i)
                if is_step(t - 1):
                    per_step(dve, probs, t - 1, i)
                    per_step(dve, pt_kept, t - 2, i)
                    nc.vector.transpose(pt_f[:, :], sc[:, (t - 1) % 2]).then_inc(turned, 1)
                small_op(image_at(t, STAT_LEAD - 1), 5, i)
                add_out(t - FINAL_LAG, 0, i)
                small_op(image_at(t, STAT_LEAD - 1), 6, i)
                add_out(t - FINAL_LAG, 1, i)
                small_op(image_at(t, STAT_LEAD - 1), 7, i)
                if is_step(t - 1):
                    per_step(dve, pt_hi, t - 1, i)
                    nc.vector.tensor_tensor(pt[:, (t - 1) % 2, 1], pt_f[:, :], pt[:, (t - 1) % 2, 0], ALU.subtract).then_inc(pt_kept, 1)
                group_squares(image_at(t, STAT_LEAD), 1, i)
                u = t + PROJ_LEAD
                if is_step(u):
                    keep_qk(u, 0, i)
                group_sums(image_at(t, RSQ_LEAD), 1, i)
                h = half_at(t, CENTRE_LEAD)
                if h is not None and h % 2 == 0:
                    per_image(dve, stats, h // 2, i, STAT_OPS)
                    per_half(dve, normed, h - 1, i)
                    centre(nc.vector, h, i)
                h = half_at(t, NORM_LEAD)
                if h is not None and h % 2 == 1:
                    normalize(h, i)
                if is_step(t):
                    per_step(dve, exped, t, i)
                    nc.vector.reduce_sum(sm[:, t % 2], rows, axis=AX.X).then_inc(row_sum, 1)
                    per_step(dve, row_sum, t, i)
                    nc.vector.reciprocal(rs[:, t % 2], sm[:, t % 2]).then_inc(inverted, 1)
                if h is not None and h % 2 == 0:
                    normalize(h, i)
                small_op(image_at(t, STAT_LEAD), 0, i)
                group_sums(image_at(t, RSUM_LEAD), 0, i)
                group_squares(image_at(t, RSQ_LEAD), 0, i)
                if is_step(u):
                    keep_qk(u, 1, i)
                small_op(image_at(t, STAT_LEAD), 1, i)

            rounds(dve, step)

        @block.gpsimd
        def _(pool):
            nc.gpsimd.memset(v_bd[:].rearrange("p a b c d e -> p (a b c d e)").bitcast(F32), 0.0).then_inc(v_zeroed, 1)

            def root(b, k, i):
                if b is None:
                    return
                if k == 0:
                    per_image(pool, stats, b, i, STAT_OPS)
                    per_half(pool, normed, 2 * b - 1, i)
                y = guess[:, :].bitcast(F32) if k == 0 else rstd[:, :]
                for n, (out_, left, right, op) in enumerate((
                        (newton, y, y, ALU.mult),
                        (newton, newton[:, :], half_var[:, :], ALU.mult),
                        (newton, three_halves[:, :], newton[:, :], ALU.subtract),
                        (rstd, y, newton[:, :], ALU.mult))):
                    wait(pool, refined, ROOT_OPS * b + 4 * k + n, i, ROOT_OPS * XBUFS)
                    nc.gpsimd.tensor_tensor(out_[:, :], left, right, op).then_inc(refined, 1)

            def root_by_token(b, i):
                if b is None:
                    return
                per_image(pool, refined, b, i, ROOT_OPS)
                c2 = WS // 2
                by_token = (CP, c2, 2 * NW, NW)
                nc.gpsimd.tensor_tensor(
                    rstd_t[:, :].rearrange("p (c x nw) -> p c x nw", c=c2, nw=NW),
                    rstd[:, :].rearrange("p (nw c) -> p c nw", c=c2).unsqueeze(2).broadcast_to(by_token),
                    x_scale[:, :].unsqueeze(1).unsqueeze(1).broadcast_to(by_token), ALU.mult).then_inc(rstd_ready, 1)

            def rest_of_values(u, i):
                if is_step(u):
                    per_step(pool, v_hi, u, i)
                    if u % 2 == 1:
                        per_step(pool, pv_done, u - 4, i)
                    nc.gpsimd.tensor_tensor(cut_values(u, 1), v_f[:, :, :], cut_values(u, 0),
                                            ALU.subtract).then_inc(v_kept, 1)

            def step(t, i):
                rows = sc[:, t % 2].rearrange("p (u c) -> p u c", c=32)
                by_row = (128, UNIT, 32)
                if is_step(t):
                    per_step(pool, maxed, t, i)
                    nc.gpsimd.tensor_tensor(rows, rows, mx[:, t % 2].unsqueeze(2).broadcast_to(by_row),
                                            ALU.subtract).then_inc(shifted, 1)
                root(image_at(t, NORM_LEAD), 2, i)
                root_by_token(image_at(t, NORM_LEAD), i)
                g = t - OUT_LAG
                if is_step(g):
                    per_step(pool, o_hi, g, i)
                    nc.gpsimd.tensor_tensor(olo[:, g % 2], o_f[:, g % 2], ohi[:, g % 2],
                                            ALU.subtract).then_inc(o_lo, 1)
                h = half_at(t, SPLIT_LEAD)
                if h is not None:
                    per_half(pool, x_hi, h, i)
                    nc.gpsimd.tensor_tensor(xlo[:, h % 2], xn[:, :, :], xhi[:, h % 2],
                                            ALU.subtract).then_inc(x_lo, 1)
                root(image_at(t, STAT_LEAD - 1), 0, i)
                rest_of_values(t + PROJ_LEAD, i)
                if is_step(t):
                    per_step(pool, inverted, t, i)
                    nc.gpsimd.tensor_tensor(rows, rows, rs[:, t % 2].unsqueeze(2).broadcast_to(by_row),
                                            ALU.mult).then_inc(probs, 1)
                root(image_at(t, STAT_LEAD - 1), 1, i)
                b = image_at(t, NORM_LEAD)
                if b is not None:
                    per_image(pool, stats, b, i, STAT_OPS)
                    per_half(pool, normed, 2 * b, i)
                    centre(nc.gpsimd, 2 * b + 1, i)

            pool.wait_ge(zeroed, 8)
            pool.wait_ge(w_absmax, 3)
            nc.gpsimd.partition_all_reduce(w_top[:, :], w_max[:, :], 128, bass.bass_isa.ReduceOp.max).then_inc(w_allmax, 1)
            rounds(pool, step)


N_WEIGHTS = 2 * CH + CH + HG * (HPG + 2 * HPG) + 2

_INS = ["x", "L0_conv_Wq", "L0_conv_Wk", "L0_conv_Wv", "L0_conv_Wo", "L0_conv_bo", "L0_conv_pos_emb", "L0_conv_scale"]


def kernel(**inputs):
    import numpy as np
    import concourse.bacc as bacc
    from concourse.bass_utils import run_bass_kernel_spmd

    nc = bacc.Bacc("TRN2", target_bir_lowering=False, num_devices=1)
    arrays, args = {}, []
    for name in _INS:
        a = np.ascontiguousarray(inputs[name])
        arrays[f"in_{name}"] = a
        args.append(nc.dram_tensor(f"in_{name}", a.shape, F32, kind="ExternalInput").ap())
    out = nc.dram_tensor("out_y", (B, C, HH, WW), F32, kind="ExternalOutput").ap()
    build(nc, *args, out)
    r = run_bass_kernel_spmd(nc, [arrays], core_ids=[0])
    return r.results[0]["out_y"]
```
